# Optimizing a Trainium2 kernel written in Bass

```python
import numpy as np
import jax
import jax.numpy as jnp

def _softmax(x, axis=-1):
    return jax.nn.softmax(x, axis=axis)

def _gelu(x):
    return jax.nn.gelu(x, approximate=True)

def _silu(x):
    return jax.nn.silu(x)

def _sigmoid(x):
    return jax.nn.sigmoid(x)

def _layernorm(x, axis=-1, eps=1e-05):
    m = jnp.mean(x, axis=axis, keepdims=True)
    v = jnp.var(x, axis=axis, keepdims=True)
    return (x - m) / jnp.sqrt(v + eps)

def _scatter_add(tgt, idx, src, axis=0):
    return tgt.at[idx].add(src)

def _segment_sum(src, seg, n):
    return jax.ops.segment_sum(src, seg, n)
kernel_name = 'mk_gnn_ffn_d2_gnn_r8_ddf3b9'

def setup_inputs(seed: int=0):
    np.random.seed(seed)
    _w = jnp.asarray

    def _rec_inputs():
        import jax
        import jax.numpy as jnp
        _gk = jax.random.key(seed)
        x = -0.0003713 + 1 * jax.random.normal(jax.random.fold_in(_gk, 1), (6250, 256), jnp.float32)
        src = jax.random.randint(jax.random.fold_in(_gk, 2), (100000,), 0, 6250, jnp.int32)
        dst = jax.random.randint(jax.random.fold_in(_gk, 3), (100000,), 0, 6250, jnp.int32)
        _o = jnp.argsort(dst, stable=True)
        src = src[_o]
        dst = dst[_o]
        edge_weight = jax.random.uniform(jax.random.fold_in(_gk, 12), (100000,), jnp.float32, 0.0, 1)
        return (x, src, dst, edge_weight)
    x, src, dst, edge_weight = _rec_inputs()

    def _L0_gnn_setup():
        import jax, jax.numpy as jnp
        import numpy as np
        N_NODES = 6250
        N_EDGES = 200000
        IN_F = 256
        OUT_F = 64
        NHEAD = 4
        ALPHA = 0.2
        key = jax.random.key(seed)
        k1, k2, k3, k4, k5 = jax.random.split(key, 5)
        x = jax.random.normal(k1, (N_NODES, IN_F), dtype=jnp.float32)
        edge_index = jax.random.randint(k2, (2, N_EDGES), 0, N_NODES, dtype=jnp.int64)
        stdv_w = np.sqrt(6.0 / (IN_F + OUT_F * NHEAD))
        W = jax.random.uniform(k3, (IN_F, OUT_F * NHEAD), dtype=jnp.float32, minval=-stdv_w, maxval=stdv_w)
        stdv_a = np.sqrt(6.0 / (NHEAD + OUT_F))
        a_l = jax.random.uniform(k4, (1, NHEAD, OUT_F), dtype=jnp.float32, minval=-stdv_a, maxval=stdv_a)
        a_r = jax.random.uniform(k5, (1, NHEAD, OUT_F), dtype=jnp.float32, minval=-stdv_a, maxval=stdv_a)
        return {'x': x, 'edge_index': edge_index, 'W': W, 'a_l': a_l, 'a_r': a_r}
    _L0_gnn_all = _L0_gnn_setup()
    _L0_gnn_in = {k: v for k, v in _L0_gnn_all.items() if k in ('W', 'a_l', 'a_r')}
    del _L0_gnn_all

    def _L0_ffn_setup():
        import jax, jax.numpy as jnp
        import numpy as np
        B, T, D, H, L = (16, 512, 256, 256, 2)

        def _lstm(x, W_ih, W_hh, b_ih, b_hh):
            x_proj = jnp.einsum('btd,gd->btg', x, W_ih) + b_ih + b_hh
            h0 = jnp.zeros((x.shape[0], W_hh.shape[1]), x.dtype)
            c0 = jnp.zeros_like(h0)

            def step(carry, xp):
                h, c = carry
                gates = xp + h @ W_hh.T
                i, f, g, o = jnp.split(gates, 4, axis=-1)
                c = jax.nn.sigmoid(f) * c + jax.nn.sigmoid(i) * jnp.tanh(g)
                h = jax.nn.sigmoid(o) * jnp.tanh(c)
                return ((h, c), h)
            _, hs = jax.lax.scan(step, (h0, c0), jnp.swapaxes(x_proj, 0, 1))
            return jnp.swapaxes(hs, 0, 1)
        key = jax.random.key(seed)
        ks = jax.random.split(key, 9)
        s = 1.0 / np.sqrt(H)
        u = lambda k, shape: jax.random.uniform(k, shape, jnp.float32, -s, s)
        return {'x': jax.random.normal(ks[0], (B, T, D), jnp.float32), 'W_ih': u(ks[1], (4 * H, D)), 'W_hh': u(ks[2], (4 * H, H)), 'b_ih': u(ks[3], (4 * H,)), 'b_hh': u(ks[4], (4 * H,)), 'W_lin': u(ks[5], (L, H)), 'b_lin': u(ks[6], (L,)), 'fw_att': jnp.full((1, H), 0.001, jnp.float32), 'bw_att': jnp.full((1, H), 0.001, jnp.float32)}
    _L0_ffn_all = _L0_ffn_setup()
    _L0_ffn_in = {k: v for k, v in _L0_ffn_all.items() if k in ('W_ih', 'W_hh', 'b_ih', 'b_hh', 'W_lin', 'b_lin', 'fw_att', 'bw_att')}
    del _L0_ffn_all

    def _L1_gnn_setup():
        import jax, jax.numpy as jnp
        import numpy as np
        N = 12500
        E = 400000
        F_IN = 256
        F_OUT = 256

        def _spmm(edge_index, edge_weight, x, n):
            dst, src = (edge_index[0], edge_index[1])
            msg = edge_weight[:, None] * x[src]
            return jax.ops.segment_sum(msg, dst, num_segments=n)
        key = jax.random.key(seed)
        k1, k2, k3, k4, k5 = jax.random.split(key, 5)
        feature = jax.random.normal(k1, (N, F_IN), dtype=jnp.float32)
        edge_index = jax.random.randint(k2, (2, E), 0, N)
        edge_weight = jax.random.uniform(k3, (E,), dtype=jnp.float32)
        stdv = 1.0 / np.sqrt(F_OUT)
        weight = jax.random.uniform(k4, (F_IN, F_OUT), dtype=jnp.float32, minval=-stdv, maxval=stdv)
        bias = jax.random.uniform(k5, (F_OUT,), dtype=jnp.float32, minval=-stdv, maxval=stdv)
        return {'feature': feature, 'edge_weight': edge_weight, 'weight': weight, 'bias': bias, 'edge_index': edge_index, 'mode': 2}
    _L1_gnn_all = _L1_gnn_setup()
    _L1_gnn_in = {k: v for k, v in _L1_gnn_all.items() if k in ('weight', 'bias')}
    del _L1_gnn_all

    def _L1_ffn_setup():
        import jax, jax.numpy as jnp
        import numpy as np
        E = 8
        K = 2
        D = 256
        H = 512
        DOUT = 256
        EPS = 1e-05
        key = jax.random.key(seed)
        ks = jax.random.split(key, 9)
        s = 0.02
        return {'x': jax.random.normal(ks[0], (4, 1024, D), jnp.float32), 'gamma': 1.0 + 0.05 * jax.random.normal(ks[1], (D,), jnp.float32), 'beta': 0.05 * jax.random.normal(ks[2], (D,), jnp.float32), 'Wr': 0.01 * jax.random.normal(ks[3], (D, E), jnp.float32), 'br': jnp.zeros((E,), jnp.float32), 'W1': s * jax.random.normal(ks[4], (E, D, H), jnp.float32), 'b1': s * jax.random.normal(ks[5], (E, H), jnp.float32), 'W2': s * jax.random.normal(ks[6], (E, H, DOUT), jnp.float32), 'b2': s * jax.random.normal(ks[7], (E, DOUT), jnp.float32)}
    _L1_ffn_all = _L1_ffn_setup()
    _L1_ffn_in = {k: v for k, v in _L1_ffn_all.items() if k in ('gamma', 'beta', 'Wr', 'br', 'W1', 'b1', 'W2', 'b2')}
    del _L1_ffn_all
    return {'x': x, 'src': src, 'dst': dst, 'edge_weight': edge_weight, 'L0_gnn_W': _L0_gnn_in['W'], 'L0_gnn_a_l': _L0_gnn_in['a_l'], 'L0_gnn_a_r': _L0_gnn_in['a_r'], 'L0_ffn_W_ih': _L0_ffn_in['W_ih'], 'L0_ffn_W_hh': _L0_ffn_in['W_hh'], 'L0_ffn_b_ih': _L0_ffn_in['b_ih'], 'L0_ffn_b_hh': _L0_ffn_in['b_hh'], 'L0_ffn_W_lin': _L0_ffn_in['W_lin'], 'L0_ffn_b_lin': _L0_ffn_in['b_lin'], 'L0_ffn_fw_att': _L0_ffn_in['fw_att'], 'L0_ffn_bw_att': _L0_ffn_in['bw_att'], 'L1_gnn_weight': _L1_gnn_in['weight'], 'L1_gnn_bias': _L1_gnn_in['bias'], 'L1_ffn_gamma': _L1_ffn_in['gamma'], 'L1_ffn_beta': _L1_ffn_in['beta'], 'L1_ffn_Wr': _L1_ffn_in['Wr'], 'L1_ffn_br': _L1_ffn_in['br'], 'L1_ffn_W1': _L1_ffn_in['W1'], 'L1_ffn_b1': _L1_ffn_in['b1'], 'L1_ffn_W2': _L1_ffn_in['W2'], 'L1_ffn_b2': _L1_ffn_in['b2']}

def reference(x, src, dst, edge_weight, L0_gnn_W, L0_gnn_a_l, L0_gnn_a_r, L0_ffn_W_ih, L0_ffn_W_hh, L0_ffn_b_ih, L0_ffn_b_hh, L0_ffn_W_lin, L0_ffn_b_lin, L0_ffn_fw_att, L0_ffn_bw_att, L1_gnn_weight, L1_gnn_bias, L1_ffn_gamma, L1_ffn_beta, L1_ffn_Wr, L1_ffn_br, L1_ffn_W1, L1_ffn_b1, L1_ffn_W2, L1_ffn_b2):
    import jax
    import jax.numpy as jnp

    def _L0_gnn_ref(x, edge_index, W, a_l, a_r):
        import jax, jax.numpy as jnp
        import numpy as np
        N_NODES = 6250
        N_EDGES = 200000
        IN_F = 256
        OUT_F = 64
        NHEAD = 4
        ALPHA = 0.2
        N = x.shape[0]
        H, F = (a_l.shape[1], a_l.shape[2])
        h = (x @ W).reshape(N, H, F)
        h = jnp.where(jnp.isnan(h), 0.0, h)
        al = jnp.sum(a_l * h, axis=-1)
        ar = jnp.sum(a_r * h, axis=-1)
        row = edge_index[0]
        col = edge_index[1]
        e = jax.nn.leaky_relu(al[row] + ar[col], negative_slope=ALPHA)
        m = jax.ops.segment_max(e, row, num_segments=N)
        m = jnp.where(jnp.isfinite(m), m, 0.0)
        ex = jnp.exp(e - m[row])
        denom = jax.ops.segment_sum(ex, row, num_segments=N)
        alpha = ex / denom[row]
        msg = alpha[:, :, None] * h[col]
        out = jax.ops.segment_sum(msg, row, num_segments=N)
        return out.reshape(N, H * F)

    def _L0_ffn_ref(x, W_ih, W_hh, b_ih, b_hh, W_lin, b_lin, fw_att, bw_att):
        import jax, jax.numpy as jnp
        import numpy as np
        B, T, D, H, L = (16, 512, 256, 256, 2)

        def _lstm(x, W_ih, W_hh, b_ih, b_hh):
            x_proj = jnp.einsum('btd,gd->btg', x, W_ih) + b_ih + b_hh
            h0 = jnp.zeros((x.shape[0], W_hh.shape[1]), x.dtype)
            c0 = jnp.zeros_like(h0)

            def step(carry, xp):
                h, c = carry
                gates = xp + h @ W_hh.T
                i, f, g, o = jnp.split(gates, 4, axis=-1)
                c = jax.nn.sigmoid(f) * c + jax.nn.sigmoid(i) * jnp.tanh(g)
                h = jax.nn.sigmoid(o) * jnp.tanh(c)
                return ((h, c), h)
            _, hs = jax.lax.scan(step, (h0, c0), jnp.swapaxes(x_proj, 0, 1))
            return jnp.swapaxes(hs, 0, 1)
        lstm_out = _lstm(x, W_ih, W_hh, b_ih, b_hh)
        logits = jnp.einsum('bth,lh->btl', lstm_out, W_lin) + b_lin
        g = jax.lax.stop_gradient(jnp.argmax(logits, axis=-1).astype(lstm_out.dtype))[..., None]
        w = g * lstm_out
        inc = jnp.cumsum(w, axis=1)
        prefix = inc - w
        suffix = inc[:, -1:, :] - inc
        return 2.0 * lstm_out + prefix * fw_att + suffix * bw_att

    def _L1_gnn_ref(feature, edge_weight, weight, bias, edge_index, mode):
        import jax, jax.numpy as jnp
        import numpy as np
        N = 12500
        E = 400000
        F_IN = 256
        F_OUT = 256

        def _spmm(edge_index, edge_weight, x, n):
            dst, src = (edge_index[0], edge_index[1])
            msg = edge_weight[:, None] * x[src]
            return jax.ops.segment_sum(msg, dst, num_segments=n)
        if mode in (1, 2):
            feature = feature - jnp.mean(feature, axis=0, keepdims=True)
        if mode == 2:
            std = jnp.std(feature, axis=0, ddof=1) + 0.0001
            feature = feature / std
        support = _spmm(edge_index, edge_weight, feature, feature.shape[0])
        output = support @ weight
        return output + bias

    def _L1_ffn_ref(x, gamma, beta, Wr, br, W1, b1, W2, b2):
        import jax, jax.numpy as jnp
        import numpy as np
        E = 8
        K = 2
        D = 256
        H = 512
        DOUT = 256
        EPS = 1e-05
        mu = jnp.mean(x, axis=-1, keepdims=True)
        var = jnp.mean(jnp.square(x - mu), axis=-1, keepdims=True)
        xn = (x - mu) * jax.lax.rsqrt(var + EPS) * gamma + beta
        logits = jnp.einsum('bsd,de->bse', xn, Wr) + br
        top_vals, top_idx = jax.lax.top_k(logits, K)
        w = jax.nn.softmax(top_vals, axis=-1)
        w_full = jnp.einsum('bsk,bske->bse', w, jax.nn.one_hot(top_idx, E, dtype=w.dtype))
        y = jnp.zeros(x.shape[:-1] + (DOUT,), x.dtype)
        for e in range(E):
            h = jax.nn.gelu(jnp.einsum('bsd,dh->bsh', xn, W1[e]) + b1[e], approximate=False)
            y_e = jnp.einsum('bsh,hd->bsd', h, W2[e]) + b2[e]
            y = y + y_e * w_full[..., e, None]
        return y
    edge_index = jnp.stack([src, dst])
    x = x + _L0_gnn_ref(_layernorm(x, axis=-1), edge_index, L0_gnn_W, L0_gnn_a_l, L0_gnn_a_r)
    x = x + _L0_ffn_ref(_layernorm(x, axis=-1)[None], L0_ffn_W_ih, L0_ffn_W_hh, L0_ffn_b_ih, L0_ffn_b_hh, L0_ffn_W_lin, L0_ffn_b_lin, L0_ffn_fw_att, L0_ffn_bw_att)[0]
    x = x + _L1_gnn_ref(_layernorm(x, axis=-1), edge_weight, L1_gnn_weight, L1_gnn_bias, edge_index, 2)
    x = x + _L1_ffn_ref(_layernorm(x, axis=-1)[None], L1_ffn_gamma, L1_ffn_beta, L1_ffn_Wr, L1_ffn_br, L1_ffn_W1, L1_ffn_b1, L1_ffn_W2, L1_ffn_b2)[0]
    return x

_drawn_inputs = setup_inputs


def setup_inputs(seed=0):
    import zlib

    import numpy as np

    out = dict(_drawn_inputs(seed))
    spreads = {'L0_ffn_fw_att': (0.0010000000474974513, 0.6),
     'L0_ffn_bw_att': (0.0010000000474974513, 0.6),
     'L1_ffn_br': (0.0, 0.343)}
    factors = {'L0_ffn_W_lin': 4.869,
     'L1_gnn_bias': 2.719,
     'L1_ffn_gamma': 8.0,
     'L1_ffn_beta': 8.0,
     'L1_ffn_b1': 21.397,
     'L1_ffn_b2': 7.095}
    for name, (base, spread) in spreads.items():
        noise = np.random.default_rng([zlib.crc32(name.encode()), seed]).standard_normal(out[name].shape)
        drawn = base * np.exp(spread * noise) if base else spread * noise
        out[name] = jnp.asarray(drawn.astype(out[name].dtype))
    for name, factor in factors.items():
        out[name] = (out[name] * factor).astype(out[name].dtype)
    return out
```

```python
from contextlib import ExitStack

import numpy as np
import concourse.bass as bass
from concourse import mybir

F32 = mybir.dt.float32
BF16 = mybir.dt.bfloat16
F16 = mybir.dt.float16
I32 = mybir.dt.int32
U32 = mybir.dt.uint32
ALU = mybir.AluOpType
ACT = mybir.ActivationFunctionType
AX = mybir.AxisListType

P = 128
N = 6250
D = 256
KD = D // P
NB = -(-N // P)
LAST = N - (NB - 1) * P
E = 100000
EC = -(-E // P)
ELAST = E - (P - 1) * EC
NK = NB + 1
NHEAD, FH = 4, 64
G = 4
NT = -(-(-(-(E + NB * (P - 1)) // P) + 1) // G) * G
PADLO = 999.0
EPS = 1e-5
BIG = 1e38
HX = D + 2 * NHEAD
MW = D + NHEAD
LO = 4096.0
GATES = 8
NE, HID = 8, 512
HC = HID // P


class Count:

    def __init__(self, sem):
        self.sem, self.base, self.n, self.it, self.per = sem, 0, 0, None, 0

    def up(self, ins):
        ins.then_inc(self.sem, 1)
        self.n += 1
        return ins

    @property
    def now(self):
        return self.base + self.n if self.it is None else self.it * self.per + (self.base + self.n)

    def enter(self, it, per, first=0):
        self.base, self.n, self.it, self.per = self.base + self.n - first * per, 0, it, per

    def leave(self, end):
        assert self.n == self.per, (self.n, self.per)
        self.base, self.n, self.it = self.base + end * self.per, 0, None


def build(nc, x, src, dst, ew, W, a_l, a_r, W_ih, W_hh, b_ih, b_hh, W_lin, b_lin, fw, bw,
          Wg, bg, gamma, beta, Wr, br, W1, b1, W2, b2, out):
    top = ExitStack()
    with top:
        def sb(name, shape, dt=F32, ctx=top):
            return ctx.enter_context(nc.sbuf_tensor(name, shape, dt))

        def sem(name):
            return top.enter_context(nc.semaphore(name))

        v, s, g, m = nc.vector, nc.scalar, nc.gpsimd, nc.tensor.matmul

        sorted_d = nc.dram_tensor("sorted_edges", (P * NT, 4), I32, kind="Internal").ap()
        ar_d = nc.dram_tensor("ar_table", (NB * P, NHEAD), F32, kind="Internal").ap()
        gat_d = nc.dram_tensor("gat_table", (NB * P, MW), F32, kind="Internal").ap()
        feat_d = nc.dram_tensor("feat_table", (NB * P, D), F32, kind="Internal").ap()

        X = sb("X", [P, NB, D])
        B = sb("B", [P, NB * MW])
        acc = B[:, :].rearrange("p (b w) -> p b w", w=MW)
        SE = sb("SE", [P, NT, 4], I32)
        ident = sb("ident", [P, P])
        ones = sb("ones", [P, P])
        iota_row = sb("iota_row", [P, P])
        tile_block = sb("tile_block", [1, NT], I32)
        stat6 = sb("stat6", [P, 2, 6])
        mv1 = sb("mv1", [P, 2])
        MV = sb("MV", [P, NB, 2])
        RS = sb("RS", [P, NB])
        rs_t = sb("rs_t", [P, NB])
        pb = [top.enter_context(nc.psum_tensor(f"bank{i}", [P, 512], F32)) for i in range(8)]

        s1_const = sem("s1_const")
        stood = {e.engine: sem(f"stood_{n}") for n, e in (("dve", nc.vector), ("pool", nc.gpsimd), ("pe", nc.tensor))}

        def stand(e, semaphore, value):
            e.wait_ge(semaphore, value)
            e.sem_inc(stood[e.engine], 1)

        def row_stats(e, c, b):
            c.up(v.bn_stats(stat6[:, 0, :], X[:, bass.ds(b, 1), :].rearrange("p b d -> p (b d)")))
            stand(e, c.sem, c.now)
            c.up(v.bn_aggr(mv1[:, :], stat6[:, 0, :]))
            e.wait_ge(c.sem, c.now)
            c.up(v.tensor_copy(MV[:, bass.ds(b, 1), :].rearrange("p b d -> p (b d)"), mv1[:, :]))
            e.wait_ge(c.sem, c.now)

        def normal(outp, xin, b):
            return v.tensor_scalar(outp, xin, MV[:, bass.ds(b, 1), 0], RS[:, bass.ds(b, 1)],
                                   ALU.subtract, ALU.mult)

        def blk(t, b):
            return t[:, bass.ds(b, 1), :].rearrange("p b d -> p (b d)")

        st = ExitStack()
        with st:
            upper = sb("upper", [P, P], ctx=st)
            upper_i = sb("upper_i", [P, P], ctx=st)
            iota_i = sb("iota_i", [P, P], I32, ctx=st)
            tiles_row = sb("tiles_row", [NK, NT], ctx=st)
            tiles_row_i = sb("tiles_row_i", [NK, NT], I32, ctx=st)
            src_i = sb("src_i", [P, EC], I32, ctx=st)
            dst_i = sb("dst_i", [P, EC], I32, ctx=st)
            ew_f = sb("ew_f", [P, EC], ctx=st)
            key_i = sb("key_i", [P, EC], I32, ctx=st)
            key = sb("key", [P, EC], ctx=st)
            rank = sb("rank", [P, EC], ctx=st)
            hot = sb("hot", [P, EC], ctx=st)
            cum = sb("cum", [P, EC], ctx=st)
            zeros = sb("zeros", [P, EC], ctx=st)
            totals = sb("totals", [P, NK], ctx=st)
            base = sb("base", [P, NK], ctx=st)
            cnt_i = sb("cnt_i", [NK, 1], I32, ctx=st)
            tiles_c = sb("tiles_c", [NK, 1], ctx=st)
            tiles_b = sb("tiles_b", [NK, P], ctx=st)
            start_r = sb("start_r", [P, NK], ctx=st)
            end_c = sb("end_c", [NK, 1], ctx=st)
            tb_f = sb("tb_f", [1, NT], ctx=st)
            pad_rec = sb("pad_rec", [P, NT, 4], I32, ctx=st)
            pos_i = sb("pos_i", [P, EC], I32, ctx=st)
            lane_i = sb("lane_i", [P, EC], I32, ctx=st)
            lane_f = sb("lane_f", [P, EC], ctx=st)
            rec = B[:, 0:EC * 5].bitcast(I32).rearrange("p (j f) -> p j f", f=5)
            rec_f = B[:, 0:EC * 5].rearrange("p (j f) -> p j f", f=5)

            s1_set = sem("s1_set")
            s1_ld = [sem(f"s1_ld{i}") for i in range(3)]
            s1_x = sem("s1_x")
            s1_pad = sem("s1_pad")
            s1_padded = sem("s1_padded")
            s1_dve = sem("s1_dve")
            s1_tot = sem("s1_tot")
            s1_cnt = sem("s1_cnt")
            s1_tiles = sem("s1_tiles")
            s1_start = sem("s1_start")
            s1_past = sem("s1_past")
            s1_blockno = sem("s1_blockno")

            with nc.Block() as block:
                @block.sync
                def _(e):
                    full = (NB - 1) * P
                    e.wait_ge(s1_set, 1)
                    e.dma_start(src_i[0:P - 1, :], src[0:(P - 1) * EC].rearrange("(p j) -> p j", j=EC)).then_inc(s1_ld[0], 16)
                    e.dma_start(src_i[P - 1:P, 0:ELAST], src[(P - 1) * EC:E].rearrange("(p j) -> p j", p=1)).then_inc(s1_ld[0], 16)
                    for f, o, a in ((1, dst_i, dst), (2, ew_f, ew)):
                        e.dma_start(o[0:P - 1, :], a[0:(P - 1) * EC].rearrange("(p j) -> p j", j=EC)).then_inc(s1_ld[f], 16)
                        e.dma_start(o[P - 1:P, 0:ELAST], a[(P - 1) * EC:E].rearrange("(p j) -> p j", p=1)).then_inc(s1_ld[f], 16)
                    e.dma_start(X[:, 0:NB - 1, :], x[0:full, :].rearrange("(b p) d -> p b d", p=P)).then_inc(s1_x, 16)
                    e.dma_start(X[0:LAST, NB - 1, :], x[full:N, :]).then_inc(s1_x, 16)
                    e.wait_ge(s1_pad, 2)
                    e.dma_start(sorted_d.rearrange("(p t) f -> p (t f)", p=P), pad_rec[:, :, :].rearrange("p t f -> p (t f)")).then_inc(s1_padded, 16)
                    e.wait_ge(s1_x, 32)
                    e.wait_ge(s1_padded, 16)

                @block.gpsimd
                def _(e):
                    g.memset(pad_rec[:, :, :], 0).then_inc(s1_pad, 1)
                    e.wait_ge(s1_pad, 1)
                    g.memset(pad_rec[:, :, 0].bitcast(F32), PADLO).then_inc(s1_pad, 1)
                    g.iota(iota_i[:, :], pattern=[[1, P]], base=0, channel_multiplier=0)
                    g.iota(tiles_row_i[:, :], pattern=[[1, NT]], base=0, channel_multiplier=0)
                    g.memset(ones[:, :], 1.0)
                    g.memset(ident[:, :], 0.0)
                    g.memset(upper[:, :], 1.0)
                    g.memset(upper_i[:, :], 1.0).then_inc(s1_const, 1)
                    e.wait_ge(s1_const, 1)
                    g.affine_select(out=ident[:, :], in_=ident[:, :], compare_op=ALU.not_equal, fill=1.0,
                                    base=0, pattern=[[-1, P]], channel_multiplier=1)
                    g.affine_select(out=upper[:, :], in_=upper[:, :], compare_op=ALU.is_ge, fill=0.0,
                                    base=-1, pattern=[[1, P]], channel_multiplier=-1)
                    g.affine_select(out=upper_i[:, :], in_=upper_i[:, :], compare_op=ALU.is_ge, fill=0.0,
                                    base=0, pattern=[[1, P]], channel_multiplier=-1).then_inc(s1_const, 1)

                @block.tensor
                def _(e):
                    e.wait_ge(s1_const, 2)
                    e.wait_ge(s1_tot, 1)
                    m(pb[0][0:NK, 0:1], totals[:, :], ones[:, 0:1], start=True, stop=True)
                    m(pb[1][:, 0:NK], upper[:, :], totals[:, :], start=True, stop=True).then_inc(s1_cnt, 1)
                    e.wait_ge(s1_tiles, 1)
                    m(pb[2][:, 0:NK], tiles_b[:, :], upper[0:NK, 0:NK], start=True, stop=True)
                    m(pb[3][0:NK, 0:1], upper_i[0:NK, 0:NK], tiles_c[:, :], start=True, stop=True).then_inc(s1_start, 1)
                    e.wait_ge(s1_past, 1)
                    half = NT // 2
                    m(pb[4][0:1, 0:half], ones[0:NK, 0:1], tiles_row[:, 0:half], start=True, stop=True)
                    m(pb[5][0:1, 0:half], ones[0:NK, 0:1], tiles_row[:, half:NT], start=True, stop=True).then_inc(s1_blockno, 1)

                @block.vector
                def _(e):
                    c = Count(s1_dve)

                    def do(ins):
                        c.up(ins)
                        e.wait_ge(c.sem, c.now)

                    do(v.memset(src_i[:, :], NB * P))
                    do(v.memset(dst_i[:, :], 0))
                    do(v.memset(ew_f[:, :], 0.0))
                    do(v.memset(rec[:, :, 3], 0))
                    v.memset(X[:, NB - 1, :], 0.0).then_inc(s1_set, 1)
                    do(v.memset(rank[:, :], 0.0))
                    do(v.memset(zeros[:, :], 0.0))
                    e.wait_ge(s1_const, 2)
                    do(v.tensor_copy(iota_row[:, :], iota_i[:, :]))
                    do(v.tensor_copy(tiles_row[:, :], tiles_row_i[:, :]))
                    e.wait_ge(s1_ld[0], 32)
                    do(v.tensor_scalar(key_i[:, :], src_i[:, :], 7, None, ALU.logical_shift_right))
                    do(v.tensor_copy(key[:, :], key_i[:, :]))
                    with e.Fori(0, NK) as k:
                        c.enter(k, 5)
                        do(v.tensor_scalar(hot[:, :], key[:, :], iota_row[:, bass.ds(k, 1)], None, ALU.is_equal))
                        do(v.tensor_tensor_scan(cum[:, :], hot[:, :], zeros[:, :], 0.0, ALU.add, ALU.add))
                        do(v.tensor_tensor(hot[:, :], hot[:, :], cum[:, :], ALU.mult))
                        c.up(v.tensor_tensor(rank[:, :], rank[:, :], hot[:, :], ALU.add))
                        do(v.tensor_copy(totals[:, bass.ds(k, 1)], cum[:, EC - 1:EC]))
                    c.leave(NK)
                    v.memset(end_c[:, :], 0.0).then_inc(s1_tot, 1)
                    e.wait_ge(s1_cnt, 1)
                    do(v.tensor_scalar(tiles_c[:, :], pb[0][0:NK, 0:1], float(P - 1), None, ALU.add))
                    do(v.tensor_copy(cnt_i[:, :], tiles_c[:, :]))
                    do(v.tensor_scalar(cnt_i[:, :], cnt_i[:, :], 7, None, ALU.logical_shift_right))
                    do(v.tensor_copy(tiles_c[:, :], cnt_i[:, :]))
                    v.tensor_copy(tiles_b[:, :], tiles_c[:, 0:1].to_broadcast([NK, P])).then_inc(s1_tiles, 1)
                    e.wait_ge(s1_start, 1)
                    do(v.tensor_scalar(start_r[:, :], pb[2][:, 0:NK], float(P), -1.0, ALU.mult, ALU.add))
                    do(v.tensor_tensor(base[:, :], start_r[:, :], pb[1][:, 0:NK], ALU.add))
                    do(v.tensor_copy(end_c[:, :], pb[3][0:NK, 0:1]))
                    v.tensor_scalar(tiles_row[:, :], tiles_row[:, :], end_c[:, 0:1], None, ALU.is_ge).then_inc(s1_past, 1)
                    with e.Fori(0, NK) as k:
                        c.enter(k, 2)
                        do(v.tensor_scalar(hot[:, :], key[:, :], iota_row[:, bass.ds(k, 1)], base[:, bass.ds(k, 1)],
                                           ALU.is_equal, ALU.mult))
                        do(v.tensor_tensor(rank[:, :], rank[:, :], hot[:, :], ALU.add))
                    c.leave(NK)
                    e.wait_ge(s1_blockno, 1)
                    half = NT // 2
                    do(v.tensor_scalar(tb_f[:, 0:half], pb[4][0:1, 0:half], float(NB - 1), None, ALU.min))
                    do(v.tensor_scalar(tb_f[:, half:NT], pb[5][0:1, 0:half], float(NB - 1), None, ALU.min))
                    do(v.tensor_copy(tile_block[:, :], tb_f[:, :]))
                    do(v.tensor_copy(pos_i[:, :], rank[:, :]))
                    do(v.tensor_scalar(lane_i[:, :], pos_i[:, :], P - 1, None, ALU.bitwise_and))
                    do(v.tensor_copy(lane_f[:, :], lane_i[:, :]))
                    do(v.tensor_scalar(pos_i[:, :], pos_i[:, :], 7, None, ALU.logical_shift_right))
                    do(v.tensor_copy(cum[:, :], pos_i[:, :]))
                    do(v.scalar_tensor_tensor(cum[:, :], lane_f[:, :], float(NT), cum[:, :], ALU.mult, ALU.add))
                    e.wait_ge(s1_ld[1], 32)
                    e.wait_ge(s1_ld[2], 32)
                    do(v.tensor_copy(rec[:, :, 1], dst_i[:, :]))
                    do(v.tensor_copy(rec_f[:, :, 2], ew_f[:, :]))
                    do(v.tensor_copy(rec[:, :, 4], cum[:, :]))
                    do(v.tensor_scalar(lane_i[:, :], src_i[:, :], P - 1, None, ALU.bitwise_and))
                    do(v.tensor_copy(lane_f[:, :], lane_i[:, :]))
                    do(v.tensor_scalar(hot[:, :], key[:, :], float(NB), PADLO, ALU.is_equal, ALU.mult))
                    do(v.tensor_tensor(rec_f[:, :, 0], lane_f[:, :], hot[:, :], ALU.add))

        ALM = sb("ALM", [P, NB, 2 * NHEAD])
        MX = sb("MX", [P, NB, NHEAD])
        st = ExitStack()
        with st:
            stage = [sb(f"stage{q}", [P, 5], I32, ctx=st) for q in range(2)]
            Wsb = sb("Wsb", [P, KD, D], ctx=st)
            a_b = sb("a_b", [P, 2, D], ctx=st)
            xn = sb("xn", [P, D], ctx=st)
            xnT = sb("xnT", [P, D], ctx=st)
            hrow = sb("hrow", [P, HX], ctx=st)
            hraw = sb("hraw", [P, D], ctx=st)
            hmask = sb("hmask", [P, D], I32, ctx=st)
            hprod = sb("hprod", [P, D], ctx=st)
            s2_w = sem("s2_w")
            s2_se = sem("s2_se")
            s2_dve = sem("s2_dve")
            s2_var = sem("s2_var")
            s2_sqrt = sem("s2_sqrt")
            s2_xn = sem("s2_xn")
            s2_t = sem("s2_t")
            s2_xnT = sem("s2_xnT")
            s2_h = sem("s2_h")
            s2_row = sem("s2_row")
            s2_st = sem("s2_st")
            s2_staged = sem("s2_staged")
            s2_sc = [sem(f"s2_sc{q}") for q in range(2)]

            with nc.Block() as block:
                @block.gpsimd
                def _(e):
                    def scatter(i, first):
                        for q in range(2):
                            if not first:
                                e.wait_ge(s2_sc[q], i * 16)
                            g.tensor_copy(stage[q][:, :], blk(rec, i * 2 + q)).then_inc(s2_staged, 1)
                            stand(e, s2_staged, i * 2 + (q + 1))
                            g.indirect_dma_start(out=sorted_d, out_offset=bass.IndirectOffsetOnAxis(ap=stage[q][:, 4:5], axis=0),
                                                 in_=stage[q][:, 0:4], in_offset=None).then_inc(s2_sc[q], 16)

                    scatter(0, True)
                    with e.Fori(1, EC // 2) as i:
                        scatter(i, False)
                    for q in range(2):
                        e.wait_ge(s2_sc[q], 16 * (EC // 2))
                    e.dma_start(SE[:, :, :].rearrange("p t f -> p (t f)"), sorted_d.rearrange("(p t) f -> p (t f)", p=P)).then_inc(s2_se, 16)
                    e.wait_ge(s2_se, 16)

                @block.sync
                def _(e):
                    e.dma_start(Wsb[:, :, :], W.rearrange("(k p) n -> p k n", p=P)).then_inc(s2_w, 16)
                    e.dma_start(a_b[:, 0, :], a_l.rearrange("a h f -> a (h f)").to_broadcast([P, D])).then_inc(s2_w, 16)
                    e.dma_start(a_b[:, 1, :], a_r.rearrange("a h f -> a (h f)").to_broadcast([P, D])).then_inc(s2_w, 16)
                    with e.Fori(0, NB) as b:
                        e.wait_ge(s2_row, b + 1)
                        e.dma_start(gat_d[bass.ds(b * P, P), :], hrow[:, 0:MW]).then_inc(s2_st, 16)
                        e.dma_start(ar_d[bass.ds(b * P, P), :], hrow[:, D:MW]).then_inc(s2_st, 16)
                    e.wait_ge(s2_st, 32 * NB)

                @block.scalar
                def _(e):
                    e.wait_ge(s2_var, 1)
                    s.activation(RS[:, :], rs_t[:, :], ACT.Sqrt).then_inc(s2_sqrt, 1)
                    with e.Fori(0, NB) as b:
                        e.wait_ge(s2_t, b + 1)
                        s.activation(xnT[:, :], pb[0][:, 0:D], ACT.Copy).then_inc(s2_xnT, 1)

                @block.tensor
                def _(e):
                    e.wait_ge(s2_w, 48)
                    with e.Fori(0, NB) as b:
                        e.wait_ge(s2_xn, b + 1)
                        for k in range(KD):
                            last = nc.tensor.transpose(pb[0][:, k * P:(k + 1) * P], xn[:, k * P:(k + 1) * P], ident[:, :])
                        last.then_inc(s2_t, 1)
                        e.wait_ge(s2_xnT, b + 1)
                        for k in range(KD):
                            last = m(pb[1][:, 0:D], xnT[:, k * P:(k + 1) * P], Wsb[:, k, :], start=k == 0, stop=k == KD - 1)
                        last.then_inc(s2_h, 1)

                @block.vector
                def _(e):
                    c = Count(s2_dve)

                    def do(ins):
                        c.up(ins)
                        e.wait_ge(c.sem, c.now)

                    with e.Fori(0, NB) as b:
                        c.enter(b, 3)
                        row_stats(e, c, b)
                    c.leave(NB)
                    do(v.tensor_scalar(rs_t[:, :], MV[:, :, 1], EPS, None, ALU.add))
                    v.reciprocal(rs_t[:, :], rs_t[:, :]).then_inc(s2_var, 1)
                    v.memset(MX[:, :, :], -BIG)
                    e.wait_ge(s2_sqrt, 1)
                    e.wait_ge(s2_w, 48)
                    def table(b, first):
                        normal(xn[:, :], blk(X, b), b).then_inc(s2_xn, 1)
                        e.wait_ge(s2_h, b + 1)
                        do(v.tensor_copy(hraw[:, :], pb[1][:, 0:D]))
                        do(v.tensor_tensor(hmask[:, :], hraw[:, :], hraw[:, :], ALU.is_equal))
                        if not first:
                            e.wait_ge(s2_st, b * 32)
                        c.up(v.memset(hrow[:, 0:D], 0.0))
                        stand(e, c.sem, c.now)
                        do(v.copy_predicated(hrow[:, 0:D], hmask[:, :], hraw[:, :]))
                        do(v.tensor_tensor(hprod[:, :], hrow[:, 0:D], a_b[:, 0, :], ALU.mult))
                        do(v.tensor_reduce(blk(ALM, b)[:, 0:NHEAD], hprod[:, :].rearrange("p (h f) -> p h f", h=NHEAD), AX.X, ALU.add))
                        do(v.tensor_tensor(hprod[:, :], hrow[:, 0:D], a_b[:, 1, :], ALU.mult))
                        v.tensor_reduce(hrow[:, D:MW], hprod[:, :].rearrange("p (h f) -> p h f", h=NHEAD), AX.X, ALU.add).then_inc(s2_row, 1)

                    table(0, True)
                    with e.Fori(1, NB) as b:
                        c.enter(b, 7, 1)
                        table(b, False)
                    c.leave(NB)
        NG = NT // G

        def groups(e, body):
            for i in range(2):
                body(i, i, i == 0, False)
            with e.Fori(1, NG // 2 - 1) as pair:
                for q in range(2):
                    body(pair * 2 + q, q, False, False)
            for i in range(NG - 2, NG):
                body(i, i % 2, False, i == NG - 1)

        def block_of(e, t):
            return e.value_load(tile_block[0:1, bass.ds(t, 1)], min_val=0, max_val=NB - 1)

        def lo(i, j):
            return SE[:, bass.ds(i * G + j, 1), 0].bitcast(F32)

        def dst_of(i):
            return SE[:, bass.ds(i * G, G), 1]

        def gather(e, i, q, slot_idx, slot, table, free, got, copied):
            if not (isinstance(i, int) and i < 2):
                e.wait_ge(free, i - 1)
            g.tensor_copy(slot_idx[q][:, :], dst_of(i)).then_inc(copied, 1)
            stand(e, copied, i + 1)
            for j in range(G):
                g.indirect_dma_start(out=slot[q][:, j, :], out_offset=None, in_=table,
                                     in_offset=bass.IndirectOffsetOnAxis(ap=slot_idx[q][:, j:j + 1], axis=0)).then_inc(got[q], 16)

        def arrived(e, got, i, q):
            e.wait_ge(got[q], 16 * G * (i // 2 + 1) if isinstance(i, int) else (i - q) * (8 * G) + 16 * G)

        st = ExitStack()
        with st:
            idx = [sb(f"ar_idx{q}", [P, G], I32, ctx=st) for q in range(2)]
            ar_e = [sb(f"ar_e{q}", [P, G, NHEAD], ctx=st) for q in range(2)]
            absent = [sb(f"absent{q}", [P, G, P], BF16, ctx=st) for q in range(2)]
            diag = [sb(f"diag{q}", [P, G, NHEAD, P], ctx=st) for q in range(2)]
            red = [sb(f"red{q}", [P, G, NHEAD], ctx=st) for q in range(2)]
            big_id = sb("big_id", [P, NHEAD, P], BF16, ctx=st)
            s3_const = sem("s3_const")
            s3_copied = sem("s3_copied")
            s3_got = [sem(f"s3_got{q}") for q in range(2)]
            s3_absent = sem("s3_absent")
            s3_diag = sem("s3_diag")
            s3_bc = sem("s3_bc")
            s3_red = sem("s3_red")
            s3_max = sem("s3_max")
            s3_m = sem("s3_m")

            with nc.Block() as block:
                @block.gpsimd
                def _(e):
                    groups(e, lambda i, q, first, last: gather(e, i, q, idx, ar_e, ar_d, s3_diag, s3_got, s3_copied))

                @block.scalar
                def _(e):
                    def body(i, q, first, last):
                        arrived(e, s3_got, i, q)
                        if not (isinstance(i, int) and i < 2):
                            e.wait_ge(s3_bc, i - 1)
                        for j in range(G):
                            for h in range(NHEAD):
                                ins = s.activation(diag[q][:, j, h, :], ident[:, :], ACT.Copy, scale=ar_e[q][:, j, h:h + 1])
                        ins.then_inc(s3_diag, 1)
                    groups(e, body)

                @block.tensor
                def _(e):
                    e.wait_ge(s3_const, 1)

                    def body(i, q, first, last):
                        if not (isinstance(i, int) and i < 2):
                            e.wait_ge(s3_red, i - 1)
                        e.wait_ge(s3_absent, i + 1)
                        e.wait_ge(s3_diag, i + 1)
                        for j in range(G):
                            m(pb[G * q + j][:, :], ones[:, :], diag[q][:, j, :, :].rearrange("p h e -> p (h e)"), start=True, stop=False)
                            ins = m(pb[G * q + j][:, :], absent[q][:, j, :], big_id[:, :, :].rearrange("p h e -> p (h e)"), start=False, stop=True)
                        ins.then_inc(s3_bc, 1)
                    groups(e, body)

                @block.vector
                def _(e):
                    v.tensor_scalar(big_id[:, :, :], ident[:, :].rearrange("p (o e) -> p o e", o=1).to_broadcast([P, NHEAD, P]), BIG, None, ALU.mult).then_inc(s3_const, 1)

                    def mark(i, q):
                        if not (isinstance(i, int) and i < 2):
                            e.wait_ge(s3_bc, i - 1)
                        for j in range(G):
                            ins = v.tensor_scalar(absent[q][:, j, :], iota_row[:, :], lo(i, j), -1.0, ALU.is_equal, ALU.add)
                        ins.then_inc(s3_absent, 1)

                    def body(i, q, first, last):
                        if first:
                            mark(i, q)
                        if not last:
                            mark(i + 1, 1 - q)
                        e.wait_ge(s3_bc, i + 1)
                        for j in range(G):
                            ins = v.tensor_reduce(red[q][:, j, :], pb[G * q + j][:, :].rearrange("p (h e) -> p h e", h=NHEAD), AX.X, ALU.max)
                        ins.then_inc(s3_red, 1)
                        e.wait_ge(s3_red, i + 1)
                        for j in range(G):
                            b = block_of(e, i * G + j)
                            if not (first and j == 0):
                                e.wait_ge(s3_max, i * G + j)
                            v.tensor_tensor(blk(MX, b), blk(MX, b), red[q][:, j, :], ALU.max).then_inc(s3_max, 1)
                    groups(e, body)
                    e.wait_ge(s3_max, NT)
                    al, mm = ALM[:, :, 0:NHEAD], ALM[:, :, NHEAD:2 * NHEAD]
                    v.tensor_tensor(mm, al, MX[:, :, :], ALU.add).then_inc(s3_m, 1)
                    e.wait_ge(s3_m, 1)
                    v.scalar_tensor_tensor(mm, mm, 0.2, mm, ALU.mult, ALU.max).then_inc(s3_m, 1)
                    v.tensor_scalar(MX[:, :, :], MX[:, :, :], -BIG / 2, None, ALU.is_gt).then_inc(s3_m, 1)
                    e.wait_ge(s3_m, 3)
                    v.tensor_tensor(mm, mm, MX[:, :, :], ALU.mult).then_inc(s3_m, 1)
                    e.wait_ge(s3_m, 4)
                    v.memset(B[:, :], 0.0)

        st = ExitStack()
        with st:
            idx = [sb(f"gat_idx{q}", [P, G], I32, ctx=st) for q in range(2)]
            msg = [sb(f"msg{q}", [P, G, MW], ctx=st) for q in range(2)]
            hot = [sb(f"hot4_{q}", [P, G, P], ctx=st) for q in range(2)]
            hotT = [sb(f"hotT{q}", [P, G, P], ctx=st) for q in range(2)]
            z = [sb(f"z{q}", [P, G, NHEAD], ctx=st) for q in range(2)]
            den = sb("den", [P, NB, NHEAD], ctx=st)
            s4_copied = sem("s4_copied")
            s4_got = [sem(f"s4_got{q}") for q in range(2)]
            s4_hot = sem("s4_hot")
            s4_T = sem("s4_T")
            s4_hotT = sem("s4_hotT")
            s4_look = sem("s4_look")
            s4_z = [sem(f"s4_z{k}") for k in range(4)]
            s4_exp = sem("s4_exp")
            s4_msg = sem("s4_msg")
            s4_sum = sem("s4_sum")
            s4_acc = sem("s4_acc")
            s4_end = sem("s4_end")
            bT, bL, bS = [pb[0], pb[1]], [pb[2], pb[3]], pb[4:8]

            with nc.Block() as block:
                @block.gpsimd
                def _(e):
                    groups(e, lambda i, q, first, last: gather(e, i, q, idx, msg, gat_d, s4_sum, s4_got, s4_copied))

                @block.scalar
                def _(e):
                    def flip(i, q):
                        e.wait_ge(s4_T, i + 1)
                        if not (isinstance(i, int) and i < 2):
                            e.wait_ge(s4_look, i - 1)
                        s.activation(hotT[q][:, :, :].rearrange("p g e -> p (g e)"), bT[q][:, :], ACT.Copy).then_inc(s4_hotT, 1)

                    def body(i, q, first, last):
                        if first:
                            flip(i, q)
                        if not last:
                            flip(i + 1, 1 - q)
                        e.wait_ge(s4_z[3], i + 1)
                        s.activation(msg[q][:, :, D:MW], z[q][:, :, :], ACT.Exp).then_inc(s4_exp, 1)
                    groups(e, body)

                @block.tensor
                def _(e):
                    def look(i, q):
                        e.wait_ge(s4_hot, i + 1)
                        for j in range(G):
                            ins = nc.tensor.transpose(bT[q][:, j * P:(j + 1) * P], hot[q][:, j, :], ident[:, :])
                        ins.then_inc(s4_T, 1)
                        e.wait_ge(s4_hotT, i + 1)
                        for j in range(G):
                            b = block_of(e, i * G + j)
                            ins = m(bL[q][:, j * 8:(j + 1) * 8], hotT[q][:, j, :], blk(ALM, b), start=True, stop=True)
                        ins.then_inc(s4_look, 1)

                    def body(i, q, first, last):
                        if first:
                            look(i, q)
                        if not last:
                            look(i + 1, 1 - q)
                        e.wait_ge(s4_msg, i + 1)
                        if not first:
                            e.wait_ge(s4_acc, i * G)
                        for j in range(G):
                            ins = m(bS[j][:, 0:MW], hot[q][:, j, :], msg[q][:, j, :], start=True, stop=True)
                        ins.then_inc(s4_sum, 1)
                    groups(e, body)

                @block.vector
                def _(e):
                    def mark(i, q):
                        if not (isinstance(i, int) and i < 2):
                            e.wait_ge(s4_sum, i - 1)
                        for j in range(G):
                            ins = v.tensor_scalar(hot[q][:, j, :], iota_row[:, :], lo(i, j), None, ALU.is_equal)
                        ins.then_inc(s4_hot, 1)

                    def take(i, q, first):
                        e.wait_ge(s4_sum, i + 1)
                        for j in range(G):
                            b = block_of(e, i * G + j)
                            if not (first and j == 0):
                                e.wait_ge(s4_acc, i * G + j)
                            v.tensor_tensor(blk(acc, b), blk(acc, b), bS[j][:, 0:MW], ALU.add).then_inc(s4_acc, 1)

                    def body(i, q, first, last):
                        if first:
                            mark(i, q)
                        if not last:
                            mark(i + 1, 1 - q)
                        look = bL[q][:, 0:G * 8].rearrange("p (g f) -> p g f", g=G)
                        arrived(e, s4_got, i, q)
                        e.wait_ge(s4_look, i + 1)
                        v.tensor_tensor(z[q][:, :, :], look[:, :, 0:NHEAD], msg[q][:, :, D:MW], ALU.add).then_inc(s4_z[0], 1)
                        e.wait_ge(s4_z[0], i + 1)
                        v.scalar_tensor_tensor(z[q][:, :, :], z[q][:, :, :], 0.2, z[q][:, :, :], ALU.mult, ALU.max).then_inc(s4_z[1], 1)
                        e.wait_ge(s4_z[1], i + 1)
                        v.tensor_tensor(z[q][:, :, :], z[q][:, :, :], look[:, :, NHEAD:2 * NHEAD], ALU.subtract).then_inc(s4_z[2], 1)
                        e.wait_ge(s4_z[2], i + 1)
                        v.tensor_scalar(z[q][:, :, :], z[q][:, :, :], 0.0, None, ALU.min).then_inc(s4_z[3], 1)
                        if not first:
                            take(i - 1, 1 - q, isinstance(i, int) and i == 1)
                        e.wait_ge(s4_exp, i + 1)
                        hm = msg[q][:, :, 0:D].rearrange("p g (h f) -> p g h f", h=NHEAD)
                        for j in range(G):
                            ins = v.tensor_tensor(hm[:, j, :, :], hm[:, j, :, :],
                                                  msg[q][:, j, D:MW].rearrange("p (h o) -> p h o", o=1).to_broadcast([P, NHEAD, FH]), ALU.mult)
                        ins.then_inc(s4_msg, 1)
                        if last:
                            take(i, q, False)
                    groups(e, body)
                    e.wait_ge(s4_acc, NT)
                    c = Count(s4_end)

                    def do(ins):
                        c.up(ins)
                        e.wait_ge(c.sem, c.now)

                    do(v.tensor_scalar(den[:, :, :], acc[:, :, D:MW], 0.5, None, ALU.max))
                    do(v.reciprocal(den[:, :, :], den[:, :, :]))
                    with e.Fori(0, NB) as b:
                        c.enter(b, 5)
                        hb = blk(acc, b)[:, 0:D].rearrange("p (h f) -> p h f", h=NHEAD)
                        do(v.tensor_tensor(hb, hb, blk(den, b).rearrange("p (h o) -> p h o", o=1).to_broadcast([P, NHEAD, FH]), ALU.mult))
                        c.up(v.tensor_tensor(blk(X, b), blk(X, b), blk(acc, b)[:, 0:D], ALU.add))
                        stand(e, c.sem, c.now)
                        row_stats(e, c, b)
                    c.leave(NB)
                    v.tensor_scalar(rs_t[:, :], MV[:, :, 1], EPS, None, ALU.add)
        hist = B[:, 0:N * KD].rearrange("p (t k) -> p t k", k=KD)
        st = ExitStack()
        with st:
            wih = sb("wih", [P, KD, GATES, P], ctx=st)
            whf = sb("whf", [P, KD, GATES, P], ctx=st)
            w_hi = sb("w_hi", [P, KD, GATES, P], F16, ctx=st)
            w_lo = sb("w_lo", [P, KD, GATES, P], F16, ctx=st)
            ident_b = sb("ident_b", [P, P], BF16, ctx=st)
            bias = sb("bias", [P, GATES], ctx=st)
            bias2 = sb("bias2", [P, GATES], ctx=st)
            xn = sb("xn5", [P, D], ctx=st)
            xnT = sb("xnT5", [P, D], ctx=st)
            xf = sb("xf", [P, P, GATES], ctx=st)
            xp = sb("xp", [P, 3, P, GATES], BF16, ctx=st)
            h_lo = sb("h_lo", [P, KD], F16, ctx=st)
            h_hi = sb("h_hi", [P, KD, 2], F16, ctx=st)
            pre = sb("pre", [P, 6], ctx=st)
            pre_o = sb("pre_o", [P, KD], ctx=st)
            sig = sb("sig", [P, 4], ctx=st)
            gc = sb("gc", [P, 4], ctx=st)
            prd = sb("prd", [P, 4], ctx=st)
            sig_o = sb("sig_o", [P, KD], ctx=st)
            tan_c = sb("tan_c", [P, KD], ctx=st)
            l5_w = sem("l5_w")
            l5_sqrt = sem("l5_sqrt")
            l5_dve = sem("l5_dve")
            l5_prep = sem("l5_prep")
            l5_xn = sem("l5_xn")
            l5_xT = sem("l5_xT")
            l5_xnT = sem("l5_xnT")
            l5_proj = sem("l5_proj")
            l5_xp = sem("l5_xp")
            gates_gif = sem("gates_gif")
            gates_o = sem("gates_o")
            pre_gif = sem("pre_gif")
            pre_o_r = sem("pre_o_r")
            act_gif = sem("act_gif")
            prods = sem("prods")
            cell = sem("cell")
            tanh_cell = sem("tanh_cell")
            h_scaled = sem("h_scaled")
            h_kept = sem("h_kept")
            h_split = sem("h_split")
            bA, bO, bX, bPr = [pb[0], pb[1]], [pb[2], pb[3]], pb[6], [pb[4], pb[5]]

            def steps(e, b, last_block, body):
                n = LAST if last_block else P
                with e.Fori(0, n // 2) as pair:
                    for q in range(2):
                        body(b * P + pair * 2 + q, pair * 2 + q, q)

            with nc.Block() as block:
                @block.sync
                def _(e):
                    e.dma_start(wih[:, :, :, :].rearrange("p k g m -> p (k g m)"), W_ih).then_inc(l5_w, 16)
                    e.dma_start(whf[:, :, :, :].rearrange("p k g m -> p (k g m)"), W_hh).then_inc(l5_w, 16)
                    e.dma_start(bias[:, :], b_ih).then_inc(l5_w, 16)
                    e.dma_start(bias2[:, :], b_hh).then_inc(l5_w, 16)
                    e.wait_ge(l5_w, 64)

                @block.scalar
                def _(e):
                    e.wait_ge(l5_dve, 1)
                    s.activation(RS[:, :], rs_t[:, :], ACT.Sqrt).then_inc(l5_sqrt, 1)
                    s.preload_act_table_set("sigmoid_and_others")

                    def step(t, u, q):
                        e.wait_ge(pre_gif, t + 1)
                        s.activation(gc[:, 0:2], pre[:, 0:2], ACT.Tanh)
                        s.activation(sig[:, :], pre[:, 2:6], ACT.Sigmoid).then_inc(act_gif, 1)
                        e.wait_ge(pre_o_r, t + 1)
                        s.activation(sig_o[:, :], pre_o[:, :], ACT.Sigmoid)
                        e.wait_ge(cell, t + 1)
                        s.activation(tan_c[:, :], gc[:, 2:4], ACT.Tanh).then_inc(tanh_cell, 1)

                    def one(b, last_block):
                        e.wait_ge(l5_xT, b + 1)
                        s.activation(xnT[:, :], bX[:, 0:D], ACT.Copy).then_inc(l5_xnT, 1)
                        steps(e, b, last_block, step)

                    with e.Fori(0, NB - 1) as b:
                        one(b, False)
                    one(NB - 1, True)

                @block.tensor
                def _(e):
                    e.wait_ge(l5_w, 64)

                    def weights(q, low):
                        for n in range(GATES):
                            bank, col = (bA[q], 2 * n) if n < 6 else (bO[q], 2 * (n - 6))
                            for k in range(KD):
                                if low:
                                    m(bank[:, col:col + 1], w_lo[:, k, n, :], h_lo[:, k:k + 1], start=False, stop=False, skip_group_check=True)
                                else:
                                    ins = m(bank[:, col:col + 2], w_hi[:, k, n, :], h_hi[:, k, :], start=False, stop=k == KD - 1, skip_group_check=True)
                            if not low and n == 5:
                                ins.then_inc(gates_gif, 1)
                        if not low:
                            ins.then_inc(gates_o, 1)

                    def one(b, last_block):
                        e.wait_ge(l5_xn, b + 1)
                        for k in range(KD):
                            ins = nc.tensor.transpose(bX[:, k * P:(k + 1) * P], xn[:, k * P:(k + 1) * P], ident[:, :])
                        ins.then_inc(l5_xT, 1)
                        e.wait_ge(l5_xnT, b + 1)
                        for n in range(GATES):
                            for k in range(KD):
                                ins = m(bPr[n // 4][:, (n % 4) * P:(n % 4 + 1) * P], wih[:, k, n, :], xnT[:, k * P:(k + 1) * P],
                                        start=k == 0, stop=k == KD - 1)
                        ins.then_inc(l5_proj, 1)
                        stand(e, l5_xp, b + 1)

                        def step(t, u, q):
                            for j in range(3):
                                m(bA[q][:, 0:12:2], ident_b[:, :], xp[:, j, bass.ds(u, 1), 0:6].rearrange("p t g -> p (t g)"),
                                  start=j == 0, stop=False, skip_group_check=True)
                            for j in range(3):
                                m(bO[q][:, 0:4:2], ident_b[:, :], xp[:, j, bass.ds(u, 1), 6:8].rearrange("p t g -> p (t g)"),
                                  start=j == 0, stop=False, skip_group_check=True)
                            e.wait_ge(h_scaled, t + 1)
                            weights(q, True)
                            e.wait_ge(h_split, t + 1)
                            weights(q, False)

                        steps(e, b, last_block, step)

                    with e.Fori(0, NB - 1) as b:
                        one(b, False)
                    one(NB - 1, True)

                @block.vector
                def _(e):
                    c = Count(l5_prep)

                    def do(ins):
                        c.up(ins)
                        e.wait_ge(c.sem, c.now)

                    v.reciprocal(rs_t[:, :], rs_t[:, :]).then_inc(l5_dve, 1)
                    do(v.tensor_copy(ident_b[:, :], ident[:, :]))
                    do(v.memset(gc[:, :], 0.0))
                    v.memset(h_lo[:, :], 0.0).then_inc(h_scaled, 1)
                    e.wait_ge(l5_w, 64)
                    do(v.tensor_tensor(bias[:, :], bias[:, :], bias2[:, :], ALU.add))
                    do(v.tensor_copy(w_hi[:, :, :, :], whf[:, :, :, :]))
                    do(v.tensor_tensor(whf[:, :, :, :], whf[:, :, :, :], w_hi[:, :, :, :], ALU.subtract))
                    do(v.tensor_scalar(w_lo[:, :, :, :], whf[:, :, :, :], LO, None, ALU.mult))
                    v.memset(h_hi[:, :, :], 0.0).then_inc(h_split, 1)
                    e.wait_ge(l5_sqrt, 1)

                    def step(t, u, q):
                        e.wait_ge(gates_gif, t + 1)
                        v.tensor_reduce(pre[:, :], bA[q][:, 0:12].rearrange("p (g j) -> p g j", j=2), AX.X, ALU.add).then_inc(pre_gif, 1)
                        e.wait_ge(gates_o, t + 1)
                        v.tensor_reduce(pre_o[:, :], bO[q][:, 0:4].rearrange("p (g j) -> p g j", j=2), AX.X, ALU.add).then_inc(pre_o_r, 1)
                        e.wait_ge(act_gif, t + 1)
                        v.tensor_tensor(prd[:, :], sig[:, :], gc[:, :], ALU.mult).then_inc(prods, 1)
                        e.wait_ge(prods, t + 1)
                        v.tensor_tensor(gc[:, 2:4], prd[:, 0:2], prd[:, 2:4], ALU.add).then_inc(cell, 1)
                        e.wait_ge(tanh_cell, t + 1)
                        hcol = hist[:, bass.ds(t, 1), :].rearrange("p t k -> p (t k)")
                        v.scalar_tensor_tensor(h_lo[:, :], sig_o[:, :], 1.0 / LO, tan_c[:, :], ALU.mult, ALU.mult).then_inc(h_scaled, 1)
                        v.tensor_tensor(hcol, sig_o[:, :], tan_c[:, :], ALU.mult).then_inc(h_kept, 1)
                        v.tensor_tensor(h_hi[:, :, 0], sig_o[:, :], tan_c[:, :], ALU.mult).then_inc(h_kept, 1)
                        e.wait_ge(h_kept, t * 2 + 2)
                        v.tensor_tensor(h_hi[:, :, 1], hcol, h_hi[:, :, 0], ALU.subtract).then_inc(h_split, 1)

                    def one(b, last_block):
                        normal(xn[:, :], blk(X, b), b).then_inc(l5_xn, 1)
                        e.wait_ge(l5_proj, b + 1)
                        for n in range(GATES):
                            c.up(v.tensor_scalar(xf[:, :, n], bPr[n // 4][:, (n % 4) * P:(n % 4 + 1) * P], bias[:, n:n + 1], None, ALU.add))
                        e.wait_ge(c.sem, c.now)
                        do(v.tensor_copy(xp[:, 0, :, :], xf[:, :, :]))
                        do(v.tensor_tensor(xf[:, :, :], xf[:, :, :], xp[:, 0, :, :], ALU.subtract))
                        do(v.tensor_copy(xp[:, 1, :, :], xf[:, :, :]))
                        do(v.tensor_tensor(xf[:, :, :], xf[:, :, :], xp[:, 1, :, :], ALU.subtract))
                        v.tensor_copy(xp[:, 2, :, :], xf[:, :, :]).then_inc(l5_xp, 1)
                        steps(e, b, last_block, step)

                    with e.Fori(0, NB - 1) as b:
                        c.enter(b, GATES + 4)
                        one(b, False)
                    c.leave(NB - 1)
                    one(NB - 1, True)

        st = ExitStack()
        with st:
            inc = sb("inc", [P, N, KD], ctx=st)
            gate = sb("gate", [P, N], BF16, ctx=st)
            wl = sb("wl", [P, KD, 2], ctx=st)
            wl_b = sb("wl_b", [P, KD, 2, P], ctx=st)
            bl = sb("bl", [P, 2], ctx=st)
            att = sb("att", [P, 2, KD], ctx=st)
            l1 = sb("l1", [P, 512], ctx=st)
            w6 = sb("w6", [P, 512, KD], ctx=st)
            t6 = sb("t6", [P, 512, KD], ctx=st)
            cp = sb("cp", [P, KD, P], ctx=st)
            s6_cp = sem("s6_cp")
            s6_w = sem("s6_w")
            s6_wb = sem("s6_wb")
            s6_logit = sem("s6_logit")
            s6_dve = sem("s6_dve")
            s6_gate = sem("s6_gate")
            s6_out = sem("s6_out")
            s6_T = sem("s6_T")
            s6_x = sem("s6_x")
            CH = 512
            NCH = N // CH
            REST = N - NCH * CH

            with nc.Block() as block:
                @block.sync
                def _(e):
                    e.dma_start(wl[:, :, :].rearrange("p k l -> p (k l)"), W_lin).then_inc(s6_w, 16)
                    e.dma_start(bl[:, :], b_lin.rearrange("(a l) -> a l", a=1).to_broadcast([P, 2])).then_inc(s6_w, 16)
                    e.dma_start(att[:, 0, :], fw).then_inc(s6_w, 16)
                    e.dma_start(att[:, 1, :], bw).then_inc(s6_w, 16)
                    e.wait_ge(s6_w, 64)

                @block.scalar
                def _(e):
                    e.wait_ge(s6_out, 1)

                    def fetch(b, n, first):
                        if not first:
                            e.wait_ge(s6_T, b)
                        s.activation(cp[:, :, 0:n].rearrange("p k t -> p t k"), hist[:, bass.ds(b * P, n), :], ACT.Copy).then_inc(s6_cp, 1)

                    fetch(0, P, True)
                    with e.Fori(1, NB - 1) as b:
                        fetch(b, P, False)
                    fetch(NB - 1, LAST, False)

                @block.tensor
                def _(e):
                    e.wait_ge(s6_wb, 1)

                    def logits(i, n, first):
                        if not first:
                            e.wait_ge(s6_gate, i)
                        for l in range(2):
                            for k in range(KD):
                                ins = m(pb[l][:, 0:n], wl_b[:, k, l, :], hist[:, bass.ds(i * CH, n), k], start=k == 0, stop=k == KD - 1)
                        ins.then_inc(s6_logit, 1)

                    logits(0, CH, True)
                    with e.Fori(1, NCH) as i:
                        logits(i, CH, False)
                    logits(NCH, REST, False)

                    def back(b, n, first):
                        e.wait_ge(s6_cp, b + 1)
                        if not first:
                            e.wait_ge(s6_x, b)
                        for k in range(KD):
                            ins = nc.tensor.transpose(pb[2][0:n, k * P:(k + 1) * P], cp[:, k, 0:n], ident[:, :])
                        ins.then_inc(s6_T, 1)

                    back(0, P, True)
                    with e.Fori(1, NB - 1) as b:
                        back(b, P, False)
                    back(NB - 1, LAST, False)

                @block.vector
                def _(e):
                    c = Count(s6_dve)

                    def do(ins):
                        c.up(ins)
                        e.wait_ge(c.sem, c.now)

                    e.wait_ge(s6_w, 64)
                    v.tensor_copy(wl_b[:, :, :, :].rearrange("p k l m -> p (k l) m"),
                                  wl[:, :, :].rearrange("p k (l o) -> p (k l) o", o=1).to_broadcast([P, KD * 2, P])).then_inc(s6_wb, 1)

                    def sums(i, n, first):
                        t0 = i * CH
                        e.wait_ge(s6_logit, i + 1)
                        do(v.tensor_scalar(l1[:, 0:n], pb[1][:, 0:n], bl[:, 1:2], None, ALU.add))
                        v.scalar_tensor_tensor(gate[:, bass.ds(t0, n)], pb[0][:, 0:n], bl[:, 0:1], l1[:, 0:n], ALU.add, ALU.is_lt).then_inc(s6_gate, 1)
                        e.wait_ge(s6_gate, i + 1)
                        for k in range(KD):
                            c.up(v.tensor_tensor(w6[:, 0:n, k], gate[:, bass.ds(t0, n)], hist[:, bass.ds(t0, n), k], ALU.mult))
                        e.wait_ge(c.sem, c.now)
                        for k in range(KD):
                            prev = 0.0 if first else inc[:, bass.ds(t0 - 1, 1), k]
                            c.up(v.tensor_tensor_scan(inc[:, bass.ds(t0, n), k], w6[:, 0:n, k], t6[:, 0:n, k], prev, ALU.add, ALU.add))
                        e.wait_ge(c.sem, c.now)

                    do(v.memset(t6[:, :, :], 0.0))
                    sums(0, CH, True)
                    with e.Fori(1, NCH) as i:
                        c.enter(i, 5, 1)
                        sums(i, CH, False)
                    c.leave(NCH)
                    sums(NCH, REST, False)

                    def outp(t0, n):
                        for k in range(KD):
                            c.up(v.tensor_tensor(w6[:, 0:n, k], gate[:, bass.ds(t0, n)], hist[:, bass.ds(t0, n), k], ALU.mult))
                        e.wait_ge(c.sem, c.now)
                        do(v.tensor_tensor(w6[:, 0:n, :], inc[:, bass.ds(t0, n), :], w6[:, 0:n, :], ALU.subtract))
                        for k in range(KD):
                            c.up(v.tensor_scalar(w6[:, 0:n, k], w6[:, 0:n, k], att[:, 0, k:k + 1], None, ALU.mult))
                            c.up(v.tensor_scalar(t6[:, 0:n, k], inc[:, bass.ds(t0, n), k], inc[:, N - 1:N, k], att[:, 2 - 1, k:k + 1], ALU.subtract, ALU.mult))
                        e.wait_ge(c.sem, c.now)
                        do(v.tensor_tensor(w6[:, 0:n, :], w6[:, 0:n, :], t6[:, 0:n, :], ALU.subtract))
                        do(v.scalar_tensor_tensor(hist[:, bass.ds(t0, n), :], hist[:, bass.ds(t0, n), :], 2.0, w6[:, 0:n, :], ALU.mult, ALU.add))

                    with e.Fori(0, NCH) as i:
                        c.enter(i, 9)
                        outp(i * CH, CH)
                    c.leave(NCH)
                    outp(NCH * CH, REST)
                    v.memset(l1[:, 0:1], 0.0).then_inc(s6_out, 1)

                    def rows(b, n):
                        e.wait_ge(s6_T, b + 1)
                        xb = blk(X, b) if n == P else X[0:n, NB - 1, :]
                        v.tensor_tensor(xb, xb, pb[2][0:n, 0:D], ALU.add).then_inc(s6_x, 1)
                        stand(e, s6_x, b + 1)
                        row_stats(e, c, b)

                    with e.Fori(0, NB - 1) as b:
                        c.enter(b, 3)
                        rows(b, P)
                    c.leave(NB - 1)
                    rows(NB - 1, LAST)
                    do(v.tensor_scalar(rs_t[:, :], MV[:, :, 1], EPS, None, ALU.add))
                    do(v.reciprocal(rs_t[:, :], rs_t[:, :]))
        featB = acc[:, :, 0:D]
        st = ExitStack()
        with st:
            mean_b = sb("mean_b", [P, D], ctx=st)
            scale_b = sb("scale_b", [P, D], ctx=st)
            sq = [sb(f"sq{q}", [P, D], ctx=st) for q in range(2)]
            s7_sqrt = sem("s7_sqrt")
            s7_f = sem("s7_f")
            s7_sum = sem("s7_sum")
            s7_mean = sem("s7_mean")
            s7_cen = sem("s7_cen")
            s7_sq = sem("s7_sq")
            s7_ssq = sem("s7_ssq")
            s7_var = sem("s7_var")
            s7_std = sem("s7_std")
            s7_dve = sem("s7_dve")
            s7_feat = sem("s7_feat")
            s7_st = sem("s7_st")

            with nc.Block() as block:
                @block.sync
                def _(e):
                    e.wait_ge(s7_feat, 1)
                    e.dma_start(feat_d.rearrange("(b p) d -> p b d", p=P), featB).then_inc(s7_st, 16)
                    e.wait_ge(s7_st, 16)

                @block.scalar
                def _(e):
                    s.activation(RS[:, :], rs_t[:, :], ACT.Sqrt).then_inc(s7_sqrt, 1)
                    e.wait_ge(s7_cen, 1)

                    def square(b, q):
                        if not (isinstance(b, int) and b < 2):
                            e.wait_ge(s7_ssq, b - 1)
                        s.activation(sq[q][:, :], blk(acc, b)[:, 0:D], ACT.Square).then_inc(s7_sq, 1)

                    square(0, 0)
                    square(1, 1)
                    with e.Fori(1, NB // 2) as i:
                        for q in range(2):
                            square(i * 2 + q, q)
                    square(NB - 1, 0)
                    e.wait_ge(s7_var, 1)
                    s.activation(scale_b[:, :], scale_b[:, :], ACT.Sqrt).then_inc(s7_std, 1)

                @block.tensor
                def _(e):
                    def total(b, start, stop):
                        e.wait_ge(s7_f, b + 1)
                        m(pb[0][:, 0:D], ones[:, :], blk(acc, b)[:, 0:D], start=start, stop=stop).then_inc(s7_sum, 1)

                    total(0, True, False)
                    with e.Fori(1, NB - 1) as b:
                        total(b, False, False)
                    total(NB - 1, False, True)

                    def squares(b, q, rows, start, stop):
                        e.wait_ge(s7_sq, b + 1)
                        m(pb[1][:, 0:D], ones[0:rows, :], sq[q][0:rows, :], start=start, stop=stop).then_inc(s7_ssq, 1)

                    squares(0, 0, P, True, False)
                    squares(1, 1, P, False, False)
                    with e.Fori(1, NB // 2) as i:
                        for q in range(2):
                            squares(i * 2 + q, q, P, False, False)
                    squares(NB - 1, 0, LAST, False, True)

                @block.vector
                def _(e):
                    e.wait_ge(s7_sqrt, 1)
                    with e.Fori(0, NB) as b:
                        normal(blk(acc, b)[:, 0:D], blk(X, b), b).then_inc(s7_f, 1)
                    e.wait_ge(s7_sum, NB)
                    v.tensor_scalar(mean_b[:, :], pb[0][:, 0:D], 1.0 / N, None, ALU.mult).then_inc(s7_mean, 1)
                    e.wait_ge(s7_mean, 1)
                    e.wait_ge(s7_f, NB)

                    def over_rows(t):
                        return t[:, :].rearrange("p (o d) -> p o d", o=1).to_broadcast([P, NB, D])

                    v.tensor_tensor(featB, featB, over_rows(mean_b), ALU.subtract).then_inc(s7_cen, 1)
                    e.wait_ge(s7_ssq, NB)
                    v.tensor_scalar(scale_b[:, :], pb[1][:, 0:D], 1.0 / (N - 1), None, ALU.mult).then_inc(s7_var, 1)
                    e.wait_ge(s7_std, 1)
                    v.tensor_scalar(scale_b[:, :], scale_b[:, :], 1e-4, None, ALU.add).then_inc(s7_dve, 1)
                    e.wait_ge(s7_dve, 1)
                    v.reciprocal(scale_b[:, :], scale_b[:, :]).then_inc(s7_dve, 1)
                    e.wait_ge(s7_dve, 2)
                    e.wait_ge(s7_cen, 1)
                    v.tensor_tensor(featB, featB, over_rows(scale_b), ALU.mult).then_inc(s7_feat, 1)
                    e.wait_ge(s7_st, 16)
                    v.memset(B[:, :], 0.0)

        st = ExitStack()
        with st:
            idx = [sb(f"f_idx{q}", [P, G], I32, ctx=st) for q in range(2)]
            fe = [sb(f"fe{q}", [P, G, D], ctx=st) for q in range(2)]
            hot = [sb(f"hot8_{q}", [P, G, P], ctx=st) for q in range(2)]
            s8_copied = sem("s8_copied")
            s8_got = [sem(f"s8_got{q}") for q in range(2)]
            s8_hot = sem("s8_hot")
            s8_sum = sem("s8_sum")
            s8_acc = sem("s8_acc")

            with nc.Block() as block:
                @block.gpsimd
                def _(e):
                    groups(e, lambda i, q, first, last: gather(e, i, q, idx, fe, feat_d, s8_sum, s8_got, s8_copied))

                @block.tensor
                def _(e):
                    def body(i, q, first, last):
                        e.wait_ge(s8_hot, i + 1)
                        arrived(e, s8_got, i, q)
                        if not (isinstance(i, int) and i < 2):
                            e.wait_ge(s8_acc, i * G - G)
                        for j in range(G):
                            ins = m(pb[G * q + j][:, 0:D], hot[q][:, j, :], fe[q][:, j, :], start=True, stop=True)
                        ins.then_inc(s8_sum, 1)
                    groups(e, body)

                @block.vector
                def _(e):
                    def mark(i, q):
                        if not (isinstance(i, int) and i < 2):
                            e.wait_ge(s8_sum, i - 1)
                        for j in range(G):
                            ins = v.tensor_scalar(hot[q][:, j, :], iota_row[:, :], lo(i, j),
                                                  SE[:, bass.ds(i * G + j, 1), 2].bitcast(F32), ALU.is_equal, ALU.mult)
                        ins.then_inc(s8_hot, 1)

                    def body(i, q, first, last):
                        if first:
                            mark(i, q)
                        if not last:
                            mark(i + 1, 1 - q)
                        e.wait_ge(s8_sum, i + 1)
                        for j in range(G):
                            b = block_of(e, i * G + j)
                            if not (first and j == 0):
                                e.wait_ge(s8_acc, i * G + j)
                            v.tensor_tensor(blk(acc, b)[:, 0:D], blk(acc, b)[:, 0:D], pb[G * q + j][:, 0:D], ALU.add).then_inc(s8_acc, 1)
                    groups(e, body)

        st = ExitStack()
        with st:
            W2sb = sb("W2sb", [P, NE * HC, D], ctx=st)
            Wrsb = sb("Wrsb", [P, KD, NE], ctx=st)
            br_b = sb("br_b", [P, NE], ctx=st)
            gam = sb("gam", [P, KD], ctx=st)
            bet = sb("bet", [P, KD], ctx=st)
            b1sb = sb("b1sb", [P, NE * HC], ctx=st)
            b2sb = sb("b2sb", [NE, D], ctx=st)
            MV2 = sb("MV2", [P, NB, 2], ctx=st)
            RS2 = sb("RS2", [P, NB], ctx=st)
            sel = sb("sel", [NE, NE, P], ctx=st)
            s9_w = sem("s9_w")
            st9 = ExitStack()
            with st9:
                Wgsb = sb("Wgsb", [P, KD, D], ctx=st9)
                bg_b = sb("bg_b", [P, D], ctx=st9)
                sup = sb("sup", [P, D], ctx=st9)
                supT = sb("supT", [P, D], ctx=st9)
                t9 = sb("t9", [P, D], ctx=st9)
                s9_g = sem("s9_g")
                s9_cp = sem("s9_cp")
                s9_T = sem("s9_T")
                s9_supT = sem("s9_supT")
                s9_o = sem("s9_o")
                s9_dve = sem("s9_dve")
                s9_free = sem("s9_free")
                s9_var = sem("s9_var")
                s9_sqrt = sem("s9_sqrt")
                s9_sel = sem("s9_sel")

                with nc.Block() as block:
                    @block.sync
                    def _(e):
                        e.dma_start(Wgsb[:, :, :], Wg.rearrange("(k p) n -> p k n", p=P)).then_inc(s9_g, 16)
                        e.dma_start(bg_b[:, :], bg.rearrange("(a n) -> a n", a=1).to_broadcast([P, D])).then_inc(s9_g, 16)
                        e.dma_start(W2sb[:, :, :], W2.rearrange("e (c p) n -> p (e c) n", p=P)).then_inc(s9_w, 16)
                        e.dma_start(Wrsb[:, :, :], Wr.rearrange("(k p) n -> p k n", p=P)).then_inc(s9_w, 16)
                        e.dma_start(br_b[:, :], br.rearrange("(a n) -> a n", a=1).to_broadcast([P, NE])).then_inc(s9_w, 16)
                        e.dma_start(gam[:, :], gamma).then_inc(s9_w, 16)
                        e.dma_start(bet[:, :], beta).then_inc(s9_w, 16)
                        e.dma_start(b1sb[:, :], b1).then_inc(s9_w, 16)
                        e.dma_start(b2sb[:, :], b2).then_inc(s9_w, 16)
                        e.wait_ge(s9_g, 32)
                        e.wait_ge(s9_w, 16 * 7)

                    @block.gpsimd
                    def _(e):
                        g.memset(sel[:, :, :], 0.0).then_inc(s9_sel, 1)
                        e.wait_ge(s9_sel, 1)
                        g.affine_select(out=sel[:, :, :], in_=sel[:, :, :], compare_op=ALU.not_equal, fill=1.0,
                                        base=0, pattern=[[-1, NE], [0, P]], channel_multiplier=1)

                    @block.scalar
                    def _(e):
                        def one(b, first):
                            if not first:
                                e.wait_ge(s9_T, b)
                            s.activation(sup[:, :], blk(acc, b)[:, 0:D], ACT.Copy).then_inc(s9_cp, 1)
                            e.wait_ge(s9_T, b + 1)
                            if not first:
                                e.wait_ge(s9_o, b)
                            s.activation(supT[:, :], pb[0][:, 0:D], ACT.Copy).then_inc(s9_supT, 1)

                        one(0, True)
                        with e.Fori(1, NB) as b:
                            one(b, False)
                        for k, r in ((1, RS), (2, RS2)):
                            e.wait_ge(s9_var, k)
                            s.activation(r[:, :], rs_t[:, :], ACT.Sqrt).then_inc(s9_sqrt, 1)

                    @block.tensor
                    def _(e):
                        e.wait_ge(s9_g, 32)

                        def one(b, first):
                            e.wait_ge(s9_cp, b + 1)
                            if not first:
                                e.wait_ge(s9_supT, b)
                            for k in range(KD):
                                ins = nc.tensor.transpose(pb[0][:, k * P:(k + 1) * P], sup[:, k * P:(k + 1) * P], ident[:, :])
                            ins.then_inc(s9_T, 1)
                            e.wait_ge(s9_supT, b + 1)
                            if not first:
                                e.wait_ge(s9_free, b)
                            for k in range(KD):
                                ins = m(pb[1][:, 0:D], supT[:, k * P:(k + 1) * P], Wgsb[:, k, :], start=k == 0, stop=k == KD - 1)
                            ins.then_inc(s9_o, 1)

                        one(0, True)
                        with e.Fori(1, NB) as b:
                            one(b, False)

                    @block.vector
                    def _(e):
                        c = Count(s9_dve)

                        def do(ins):
                            c.up(ins)
                            e.wait_ge(c.sem, c.now)

                        e.wait_ge(s9_g, 32)
                        with e.Fori(0, NB) as b:
                            c.enter(b, 4)
                            e.wait_ge(s9_o, b + 1)
                            v.tensor_tensor(t9[:, :], pb[1][:, 0:D], bg_b[:, :], ALU.add).then_inc(s9_free, 1)
                            e.wait_ge(s9_free, b + 1)
                            c.up(v.tensor_tensor(blk(X, b), blk(X, b), t9[:, :], ALU.add))
                            stand(e, c.sem, c.now)
                            row_stats(e, c, b)
                        c.leave(NB)
                        do(v.tensor_scalar(rs_t[:, :], MV[:, :, 1], EPS, None, ALU.add))
                        v.reciprocal(rs_t[:, :], rs_t[:, :]).then_inc(s9_var, 1)
                        e.wait_ge(s9_sqrt, 1)
                        with e.Fori(0, NB) as b:
                            c.enter(b, 4)
                            do(normal(t9[:, :], blk(X, b), b))
                            c.up(v.bn_stats(stat6[:, 0, :], t9[:, :]))
                            stand(e, c.sem, c.now)
                            do(v.bn_aggr(mv1[:, :], stat6[:, 0, :]))
                            do(v.tensor_copy(blk(MV2, b), mv1[:, :]))
                        c.leave(NB)
                        do(v.tensor_scalar(rs_t[:, :], MV2[:, :, 1], EPS, None, ALU.add))
                        v.reciprocal(rs_t[:, :], rs_t[:, :]).then_inc(s9_var, 1)

            W1sb = B[:, 0:NE * KD * HID].rearrange("p (e k n) -> p e k n", e=NE, k=KD)
            xn4 = sb("xn4", [P, G, D], ctx=st)
            xnT = sb("xnT10", [P, KD, G * P], ctx=st)
            lg = sb("lg", [P, G, NE], ctx=st)
            mx8 = sb("mx8", [P, G, 8], ctx=st)
            ix8 = sb("ix8", [P, G, 8], U32, ctx=st)
            ixf = sb("ixf", [P, G, 8], ctx=st)
            d21 = sb("d21", [P, G, 1], ctx=st)
            wts = sb("wts", [P, G, 2], ctx=st)
            wf = sb("wf", [P, G, NE], ctx=st)
            wf2 = sb("wf2", [P, G, NE], ctx=st)
            wT = sb("wT", [NE, G * P], ctx=st)
            hT = [sb(f"hT{q}", [P, G * P], ctx=st) for q in range(2)]
            yS = sb("yS", [P, KD, G * P], ctx=st)
            t_w1 = sem("t_w1")
            t_dve = sem("t_dve")
            t_xn = sem("t_xn")
            t_T = sem("t_T")
            t_xnT = sem("t_xnT")
            t_lg = sem("t_lg")
            t_d21 = sem("t_d21")
            t_exp = sem("t_exp")
            t_wf = sem("t_wf")
            t_wTp = sem("t_wTp")
            t_wT = sem("t_wT")
            t_wb = sem("t_wb")
            t_H = sem("t_H")
            t_gelu = sem("t_gelu")
            t_hw = sem("t_hw")
            t_Y = sem("t_Y")
            t_yS = sem("t_yS")
            t_back = sem("t_back")
            t_x = sem("t_x")
            t_out = sem("t_out")
            NU = NE * HC
            bH, bW, bY, bL, bwT = [pb[0], pb[1]], [pb[2], pb[3]], [pb[4], pb[5]], pb[6], pb[7]
            NGB = NB // G
            assert NB == NGB * G + 1

            with nc.Block() as block:
                @block.sync
                def _(e):
                    e.dma_start(W1sb, W1.rearrange("e (k p) n -> p e k n", p=P)).then_inc(t_w1, 16)
                    with e.Fori(0, NGB) as i:
                        e.wait_ge(t_x, i + 1)
                        e.dma_start(out[bass.ds(i * (G * P), G * P), :].rearrange("(b p) d -> p b d", p=P), X[:, bass.ds(i * G, G), :]).then_inc(t_out, 16)
                    e.wait_ge(t_x, NGB + 1)
                    e.dma_start(out[(NB - 1) * P:N, :], X[0:LAST, NB - 1, :]).then_inc(t_out, 16)
                    e.wait_ge(t_out, 16 * (NGB + 1))
                    e.wait_ge(t_w1, 16)

                @block.scalar
                def _(e):
                    def body(i, nb):
                        n = nb * P
                        e.wait_ge(t_d21, i + 1)
                        s.activation(wts[:, 0:nb, 1:2], d21[:, 0:nb, :], ACT.Exp).then_inc(t_exp, 1)
                        e.wait_ge(t_wTp, i + 1)
                        s.activation(wT[:, 0:n], bwT[0:NE, 0:n], ACT.Copy).then_inc(t_wT, 1)
                        for u in range(NU):
                            e.wait_ge(t_H, i * NU + (u + 1))
                            if not (isinstance(i, int) and i == 0 and u < 2):
                                e.wait_ge(t_Y, i * NU + (u - 1))
                            s.activation(hT[u % 2][:, 0:n], bH[u % 2][:, 0:n], ACT.Gelu, bias=b1sb[:, u:u + 1]).then_inc(t_gelu, 1)
                        e.wait_ge(t_Y, i * NU + NU)
                        s.activation(yS[:, 0, 0:n], bY[0][:, 0:n], ACT.Copy)
                        s.activation(yS[:, 1, 0:n], bY[1][:, 0:n], ACT.Copy).then_inc(t_yS, 1)

                    body(0, G)
                    with e.Fori(1, NGB) as i:
                        body(i, G)
                    body(NGB, 1)

                @block.tensor
                def _(e):
                    e.wait_ge(t_w1, 16)

                    def body(i, nb):
                        n = nb * P
                        e.wait_ge(t_xn, i + 1)
                        for k in range(KD):
                            for r in range(nb):
                                ins = nc.tensor.transpose(bH[k][:, r * P:(r + 1) * P], xn4[:, r, k * P:(k + 1) * P], ident[:, :])
                        ins.then_inc(t_T, 1)
                        e.wait_ge(t_xnT, i + 1)
                        for r in range(nb):
                            for k in range(KD):
                                ins = m(bL[:, r * NE:(r + 1) * NE], xnT[:, k, r * P:(r + 1) * P], Wrsb[:, k, :], start=k == 0, stop=k == KD - 1)
                        ins.then_inc(t_lg, 1)
                        e.wait_ge(t_wf, i + 1)
                        for r in range(nb):
                            ins = nc.tensor.transpose(bwT[0:NE, r * P:(r + 1) * P], wf[:, r, :], ident[:, :])
                        ins.then_inc(t_wTp, 1)
                        e.wait_ge(t_wT, i + 1)
                        for d in range(KD):
                            m(bY[d][:, 0:n], b2sb[:, d * P:(d + 1) * P], wT[:, 0:n], start=True, stop=False, skip_group_check=True)

                        def down(u):
                            e.wait_ge(t_hw, i * NU + (u + 1))
                            for d in range(KD):
                                ins = m(bY[d][:, 0:n], W2sb[:, u, d * P:(d + 1) * P], hT[u % 2][:, 0:n], start=False, stop=u == NU - 1, skip_group_check=True)
                            ins.then_inc(t_Y, 1)

                        for u in range(NU):
                            x_, hc = u // HC, u % HC
                            if hc == 0:
                                m(bW[x_ % 2][:, 0:n], sel[:, x_, :], wT[:, 0:n], start=True, stop=True).then_inc(t_wb, 1)
                            if u >= 2:
                                e.wait_ge(t_gelu, i * NU + (u - 1))
                            for k in range(KD):
                                ins = m(bH[u % 2][:, 0:n], W1sb[:, x_, k, hc * P:(hc + 1) * P], xnT[:, k, 0:n], start=k == 0, stop=k == KD - 1)
                            ins.then_inc(t_H, 1)
                            if u >= 1:
                                down(u - 1)
                        down(NU - 1)
                        e.wait_ge(t_yS, i + 1)
                        for r in range(nb):
                            for d in range(KD):
                                ins = nc.tensor.transpose(bH[r // 2][:, (r % 2) * D + d * P:(r % 2) * D + (d + 1) * P], yS[:, d, r * P:(r + 1) * P], ident[:, :])
                        ins.then_inc(t_back, 1)

                    body(0, G)
                    with e.Fori(1, NGB) as i:
                        body(i, G)
                    body(NGB, 1)

                @block.vector
                def _(e):
                    c = Count(t_dve)

                    def do(ins):
                        c.up(ins)
                        e.wait_ge(c.sem, c.now)

                    def body(i, nb):
                        n = nb * P
                        for r in range(nb):
                            b = i * G + r
                            c.up(normal(xn4[:, r, :], blk(X, b), b))
                        e.wait_ge(c.sem, c.now)
                        for r in range(nb):
                            b = i * G + r
                            ins = v.tensor_scalar(xn4[:, r, :], xn4[:, r, :], MV2[:, bass.ds(b, 1), 0], RS2[:, bass.ds(b, 1)], ALU.subtract, ALU.mult)
                        ins.then_inc(t_xn, 1)
                        e.wait_ge(t_T, i + 1)
                        for k in range(KD):
                            ins = v.tensor_scalar(xnT[:, k, 0:n], bH[k][:, 0:n], gam[:, k:k + 1], bet[:, k:k + 1], ALU.mult, ALU.add)
                        ins.then_inc(t_xnT, 1)
                        e.wait_ge(t_lg, i + 1)
                        do(v.tensor_tensor(lg[:, 0:nb, :], bL[:, 0:nb * NE].rearrange("p (r x) -> p r x", r=nb),
                                           br_b[:, :].rearrange("p (o x) -> p o x", o=1).to_broadcast([P, nb, NE]), ALU.add))
                        stand(e, c.sem, c.now)
                        for r in range(nb):
                            c.up(v.max(mx8[:, r, :], lg[:, r, :]))
                        stand(e, c.sem, c.now)
                        for r in range(nb):
                            c.up(v.max_index(ix8[:, r, :], mx8[:, r, :], lg[:, r, :]))
                        v.tensor_tensor(d21[:, 0:nb, :], mx8[:, 0:nb, 1:2], mx8[:, 0:nb, 0:1], ALU.subtract).then_inc(t_d21, 1)
                        e.wait_ge(c.sem, c.now)
                        do(v.tensor_copy(ixf[:, 0:nb, :], ix8[:, 0:nb, :]))
                        e.wait_ge(t_exp, i + 1)
                        do(v.tensor_scalar(wts[:, 0:nb, 0:1], wts[:, 0:nb, 1:2], 1.0, None, ALU.add))
                        do(v.reciprocal(wts[:, 0:nb, 0:1], wts[:, 0:nb, 0:1]))
                        do(v.tensor_tensor(wts[:, 0:nb, 1:2], wts[:, 0:nb, 1:2], wts[:, 0:nb, 0:1], ALU.mult))
                        for r in range(nb):
                            c.up(v.tensor_scalar(wf[:, r, :], iota_row[:, 0:NE], ixf[:, r, 0:1], wts[:, r, 0:1], ALU.is_equal, ALU.mult))
                            c.up(v.tensor_scalar(wf2[:, r, :], iota_row[:, 0:NE], ixf[:, r, 1:2], wts[:, r, 1:2], ALU.is_equal, ALU.mult))
                        e.wait_ge(c.sem, c.now)
                        v.tensor_tensor(wf[:, 0:nb, :], wf[:, 0:nb, :], wf2[:, 0:nb, :], ALU.add).then_inc(t_wf, 1)
                        for u in range(NU):
                            if u % HC == 0:
                                e.wait_ge(t_wb, i * NE + (u // HC + 1))
                            e.wait_ge(t_gelu, i * NU + (u + 1))
                            v.tensor_tensor(hT[u % 2][:, 0:n], hT[u % 2][:, 0:n], bW[(u // HC) % 2][:, 0:n], ALU.mult).then_inc(t_hw, 1)
                        e.wait_ge(t_back, i + 1)
                        for r in range(nb):
                            xb = blk(X, i * G + r)
                            ins = v.tensor_tensor(xb, xb, bH[r // 2][:, (r % 2) * D:(r % 2 + 1) * D], ALU.add)
                        ins.then_inc(t_x, 1)

                    per = G + 1 + G + G + 1 + 3 + 2 * G
                    body(0, G)
                    with e.Fori(1, NGB) as i:
                        c.enter(i, per, 1)
                        body(i, G)
                    c.leave(NGB)
                    body(NGB, 1)


_INS = ["x", "src", "dst", "edge_weight", "L0_gnn_W", "L0_gnn_a_l", "L0_gnn_a_r", "L0_ffn_W_ih", "L0_ffn_W_hh",
        "L0_ffn_b_ih", "L0_ffn_b_hh", "L0_ffn_W_lin", "L0_ffn_b_lin", "L0_ffn_fw_att", "L0_ffn_bw_att",
        "L1_gnn_weight", "L1_gnn_bias", "L1_ffn_gamma", "L1_ffn_beta", "L1_ffn_Wr", "L1_ffn_br",
        "L1_ffn_W1", "L1_ffn_b1", "L1_ffn_W2", "L1_ffn_b2"]


GATE_ORDER = (2, 0, 1, 3)


def _columns(w):
    w = np.concatenate([w[i * D:(i + 1) * D] for i in GATE_ORDER])
    return w.T.reshape(KD, P, GATES, P).transpose(1, 0, 2, 3).reshape(P, KD * GATES * P)


def _halves(a):
    return np.asarray(a).reshape(-1, P).T


def _laid_out(inputs):
    a = {n: np.asarray(inputs[n]) for n in _INS}
    for n in ("L0_ffn_W_ih", "L0_ffn_W_hh"):
        a[n] = _columns(a[n])
    for n in ("L0_ffn_b_ih", "L0_ffn_b_hh"):
        a[n] = _halves(np.concatenate([a[n][i * D:(i + 1) * D] for i in GATE_ORDER]))
    a["L0_ffn_W_lin"] = a["L0_ffn_W_lin"].T.reshape(KD, P, 2).transpose(1, 0, 2).reshape(P, KD * 2)
    for n in ("L0_ffn_fw_att", "L0_ffn_bw_att", "L1_ffn_gamma", "L1_ffn_beta"):
        a[n] = _halves(a[n].reshape(-1))
    a["L1_ffn_b1"] = _halves(a["L1_ffn_b1"].reshape(-1))
    return {n: np.ascontiguousarray(b) for n, b in a.items()}

def kernel(**inputs):
    import concourse.bacc as _bacc
    from concourse import mybir as _mybir
    from concourse.bass_utils import run_bass_kernel_spmd as _run

    nc = _bacc.Bacc("TRN2", target_bir_lowering=False, num_devices=1)
    arrays, args = {}, []
    for name, a in _laid_out(inputs).items():
        arrays[f"in_{name}"] = a
        args.append(nc.dram_tensor(f"in_{name}", a.shape, _mybir.dt.from_np(a.dtype), kind="ExternalInput").ap())
    out = nc.dram_tensor("out_0", (N, D), F32, kind="ExternalOutput").ap()
    build(nc, *args, out)
    r = _run(nc, [arrays], core_ids=[0])
    return r.results[0]["out_0"]
```

```python
from contextlib import ExitStack

import numpy as np
import concourse.bass as bass
from concourse import mybir

F32 = mybir.dt.float32
BF16 = mybir.dt.bfloat16
F16 = mybir.dt.float16
I32 = mybir.dt.int32
U32 = mybir.dt.uint32
ALU = mybir.AluOpType
ACT = mybir.ActivationFunctionType
AX = mybir.AxisListType

P = 128
N = 6250
D = 256
KD = D // P
NB = -(-N // P)
LAST = N - (NB - 1) * P
E = 100000
EC = -(-E // P)
ELAST = E - (P - 1) * EC
NK = NB + 1
NHEAD, FH = 4, 64
G = 4
NT = -(-(-(-(E + NB * (P - 1)) // P) + 1) // G) * G
PADLO = 999.0
EPS = 1e-5
BIG = 1e38
HX = D + 2 * NHEAD
MW = D + NHEAD
GATES = 8
W_SCALE = 64.0
SUMS = 5
NE, HID = 8, 512
HC = HID // P


class Count:

    def __init__(self, sem):
        self.sem, self.base, self.n, self.it, self.per = sem, 0, 0, None, 0

    def up(self, ins):
        ins.then_inc(self.sem, 1)
        self.n += 1
        return ins

    @property
    def now(self):
        return self.base + self.n if self.it is None else self.it * self.per + (self.base + self.n)

    def enter(self, it, per, first=0):
        self.base, self.n, self.it, self.per = self.base + self.n - first * per, 0, it, per

    def leave(self, end):
        assert self.n == self.per, (self.n, self.per)
        self.base, self.n, self.it = self.base + end * self.per, 0, None


def build(nc, x, src, dst, ew, W, a_l, a_r, W_ih, W_hh, b_ih, b_hh, W_lin, b_lin, fw, bw,
          Wg, bg, gamma, beta, Wr, br, W1, b1, W2, b2, out):
    top = ExitStack()
    with top:
        def sb(name, shape, dt=F32, ctx=top):
            return ctx.enter_context(nc.sbuf_tensor(name, shape, dt))

        def sem(name):
            return top.enter_context(nc.semaphore(name))

        v, s, g, m = nc.vector, nc.scalar, nc.gpsimd, nc.tensor.matmul

        sorted_d = nc.dram_tensor("sorted_edges", (P * NT, 4), I32, kind="Internal").ap()
        ar_d = nc.dram_tensor("ar_table", (NB * P, NHEAD), F32, kind="Internal").ap()
        gat_d = nc.dram_tensor("gat_table", (NB * P, MW), F32, kind="Internal").ap()
        feat_d = nc.dram_tensor("feat_table", (NB * P, D), F32, kind="Internal").ap()

        X = sb("X", [P, NB, D])
        B = sb("B", [P, NB * MW])
        acc = B[:, :].rearrange("p (b w) -> p b w", w=MW)
        SE = sb("SE", [P, NT, 4], I32)
        ident = sb("ident", [P, P])
        ones = sb("ones", [P, P])
        iota_row = sb("iota_row", [P, P])
        tile_block = sb("tile_block", [1, NT], I32)
        stat6 = sb("stat6", [P, 2, 6])
        mv1 = sb("mv1", [P, 2])
        MV = sb("MV", [P, NB, 2])
        RS = sb("RS", [P, NB])
        rs_t = sb("rs_t", [P, NB])
        pb = [top.enter_context(nc.psum_tensor(f"bank{i}", [P, 512], F32)) for i in range(8)]

        s1_const = sem("s1_const")
        stood = {e.engine: sem(f"stood_{n}") for n, e in (("dve", nc.vector), ("pool", nc.gpsimd), ("pe", nc.tensor))}

        def stand(e, semaphore, value):
            e.wait_ge(semaphore, value)
            e.sem_inc(stood[e.engine], 1)

        def row_stats(e, c, b):
            c.up(v.bn_stats(stat6[:, 0, :], X[:, bass.ds(b, 1), :].rearrange("p b d -> p (b d)")))
            stand(e, c.sem, c.now)
            c.up(v.bn_aggr(mv1[:, :], stat6[:, 0, :]))
            e.wait_ge(c.sem, c.now)
            c.up(v.tensor_copy(MV[:, bass.ds(b, 1), :].rearrange("p b d -> p (b d)"), mv1[:, :]))
            e.wait_ge(c.sem, c.now)

        def normal(outp, xin, b):
            return v.tensor_scalar(outp, xin, MV[:, bass.ds(b, 1), 0], RS[:, bass.ds(b, 1)],
                                   ALU.subtract, ALU.mult)

        def blk(t, b):
            return t[:, bass.ds(b, 1), :].rearrange("p b d -> p (b d)")

        st = ExitStack()
        with st:
            upper = sb("upper", [P, P], ctx=st)
            upper_i = sb("upper_i", [P, P], ctx=st)
            iota_i = sb("iota_i", [P, P], I32, ctx=st)
            tiles_row = sb("tiles_row", [NK, NT], ctx=st)
            tiles_row_i = sb("tiles_row_i", [NK, NT], I32, ctx=st)
            src_i = sb("src_i", [P, EC], I32, ctx=st)
            dst_i = sb("dst_i", [P, EC], I32, ctx=st)
            ew_f = sb("ew_f", [P, EC], ctx=st)
            key_i = sb("key_i", [P, EC], I32, ctx=st)
            key = sb("key", [P, EC], ctx=st)
            rank = sb("rank", [P, EC], ctx=st)
            hot = sb("hot", [P, EC], ctx=st)
            cum = sb("cum", [P, EC], ctx=st)
            zeros = sb("zeros", [P, EC], ctx=st)
            totals = sb("totals", [P, NK], ctx=st)
            base = sb("base", [P, NK], ctx=st)
            cnt_i = sb("cnt_i", [NK, 1], I32, ctx=st)
            tiles_c = sb("tiles_c", [NK, 1], ctx=st)
            tiles_b = sb("tiles_b", [NK, P], ctx=st)
            start_r = sb("start_r", [P, NK], ctx=st)
            end_c = sb("end_c", [NK, 1], ctx=st)
            tb_f = sb("tb_f", [1, NT], ctx=st)
            pad_rec = sb("pad_rec", [P, NT, 4], I32, ctx=st)
            pos_i = sb("pos_i", [P, EC], I32, ctx=st)
            lane_i = sb("lane_i", [P, EC], I32, ctx=st)
            lane_f = sb("lane_f", [P, EC], ctx=st)
            rec = B[:, 0:EC * 5].bitcast(I32).rearrange("p (j f) -> p j f", f=5)
            rec_f = B[:, 0:EC * 5].rearrange("p (j f) -> p j f", f=5)

            s1_set = sem("s1_set")
            s1_ld = [sem(f"s1_ld{i}") for i in range(3)]
            s1_x = sem("s1_x")
            s1_pad = sem("s1_pad")
            s1_padded = sem("s1_padded")
            s1_dve = sem("s1_dve")
            s1_tot = sem("s1_tot")
            s1_cnt = sem("s1_cnt")
            s1_tiles = sem("s1_tiles")
            s1_start = sem("s1_start")
            s1_past = sem("s1_past")
            s1_blockno = sem("s1_blockno")

            with nc.Block() as block:
                @block.sync
                def _(e):
                    full = (NB - 1) * P
                    e.wait_ge(s1_set, 1)
                    e.dma_start(src_i[0:P - 1, :], src[0:(P - 1) * EC].rearrange("(p j) -> p j", j=EC)).then_inc(s1_ld[0], 16)
                    e.dma_start(src_i[P - 1:P, 0:ELAST], src[(P - 1) * EC:E].rearrange("(p j) -> p j", p=1)).then_inc(s1_ld[0], 16)
                    for f, o, a in ((1, dst_i, dst), (2, ew_f, ew)):
                        e.dma_start(o[0:P - 1, :], a[0:(P - 1) * EC].rearrange("(p j) -> p j", j=EC)).then_inc(s1_ld[f], 16)
                        e.dma_start(o[P - 1:P, 0:ELAST], a[(P - 1) * EC:E].rearrange("(p j) -> p j", p=1)).then_inc(s1_ld[f], 16)
                    e.dma_start(X[:, 0:NB - 1, :], x[0:full, :].rearrange("(b p) d -> p b d", p=P)).then_inc(s1_x, 16)
                    e.dma_start(X[0:LAST, NB - 1, :], x[full:N, :]).then_inc(s1_x, 16)
                    e.wait_ge(s1_pad, 2)
                    e.dma_start(sorted_d.rearrange("(p t) f -> p (t f)", p=P), pad_rec[:, :, :].rearrange("p t f -> p (t f)")).then_inc(s1_padded, 16)
                    e.wait_ge(s1_x, 32)
                    e.wait_ge(s1_padded, 16)

                @block.gpsimd
                def _(e):
                    g.memset(pad_rec[:, :, :], 0).then_inc(s1_pad, 1)
                    e.wait_ge(s1_pad, 1)
                    g.memset(pad_rec[:, :, 0].bitcast(F32), PADLO).then_inc(s1_pad, 1)
                    g.iota(iota_i[:, :], pattern=[[1, P]], base=0, channel_multiplier=0)
                    g.iota(tiles_row_i[:, :], pattern=[[1, NT]], base=0, channel_multiplier=0)
                    g.memset(ones[:, :], 1.0)
                    g.memset(ident[:, :], 0.0)
                    g.memset(upper[:, :], 1.0)
                    g.memset(upper_i[:, :], 1.0).then_inc(s1_const, 1)
                    e.wait_ge(s1_const, 1)
                    g.affine_select(out=ident[:, :], in_=ident[:, :], compare_op=ALU.not_equal, fill=1.0,
                                    base=0, pattern=[[-1, P]], channel_multiplier=1)
                    g.affine_select(out=upper[:, :], in_=upper[:, :], compare_op=ALU.is_ge, fill=0.0,
                                    base=-1, pattern=[[1, P]], channel_multiplier=-1)
                    g.affine_select(out=upper_i[:, :], in_=upper_i[:, :], compare_op=ALU.is_ge, fill=0.0,
                                    base=0, pattern=[[1, P]], channel_multiplier=-1).then_inc(s1_const, 1)

                @block.tensor
                def _(e):
                    e.wait_ge(s1_const, 2)
                    e.wait_ge(s1_tot, 1)
                    m(pb[0][0:NK, 0:1], totals[:, :], ones[:, 0:1], start=True, stop=True)
                    m(pb[1][:, 0:NK], upper[:, :], totals[:, :], start=True, stop=True).then_inc(s1_cnt, 1)
                    e.wait_ge(s1_tiles, 1)
                    m(pb[2][:, 0:NK], tiles_b[:, :], upper[0:NK, 0:NK], start=True, stop=True)
                    m(pb[3][0:NK, 0:1], upper_i[0:NK, 0:NK], tiles_c[:, :], start=True, stop=True).then_inc(s1_start, 1)
                    e.wait_ge(s1_past, 1)
                    half = NT // 2
                    m(pb[4][0:1, 0:half], ones[0:NK, 0:1], tiles_row[:, 0:half], start=True, stop=True)
                    m(pb[5][0:1, 0:half], ones[0:NK, 0:1], tiles_row[:, half:NT], start=True, stop=True).then_inc(s1_blockno, 1)

                @block.vector
                def _(e):
                    c = Count(s1_dve)

                    def do(ins):
                        c.up(ins)
                        e.wait_ge(c.sem, c.now)

                    do(v.memset(src_i[:, :], NB * P))
                    do(v.memset(dst_i[:, :], 0))
                    do(v.memset(ew_f[:, :], 0.0))
                    do(v.memset(rec[:, :, 3], 0))
                    v.memset(X[:, NB - 1, :], 0.0).then_inc(s1_set, 1)
                    do(v.memset(rank[:, :], 0.0))
                    do(v.memset(zeros[:, :], 0.0))
                    e.wait_ge(s1_const, 2)
                    do(v.tensor_copy(iota_row[:, :], iota_i[:, :]))
                    do(v.tensor_copy(tiles_row[:, :], tiles_row_i[:, :]))
                    e.wait_ge(s1_ld[0], 32)
                    do(v.tensor_scalar(key_i[:, :], src_i[:, :], 7, None, ALU.logical_shift_right))
                    do(v.tensor_copy(key[:, :], key_i[:, :]))
                    with e.Fori(0, NK) as k:
                        c.enter(k, 5)
                        do(v.tensor_scalar(hot[:, :], key[:, :], iota_row[:, bass.ds(k, 1)], None, ALU.is_equal))
                        do(v.tensor_tensor_scan(cum[:, :], hot[:, :], zeros[:, :], 0.0, ALU.add, ALU.add))
                        do(v.tensor_tensor(hot[:, :], hot[:, :], cum[:, :], ALU.mult))
                        c.up(v.tensor_tensor(rank[:, :], rank[:, :], hot[:, :], ALU.add))
                        do(v.tensor_copy(totals[:, bass.ds(k, 1)], cum[:, EC - 1:EC]))
                    c.leave(NK)
                    v.tensor_copy(end_c[:, :], iota_row[0:NK, 0:1]).then_inc(s1_tot, 1)
                    e.wait_ge(s1_cnt, 1)
                    do(v.tensor_scalar(tiles_c[:, :], pb[0][0:NK, 0:1], float(P - 1), None, ALU.add))
                    do(v.tensor_copy(cnt_i[:, :], tiles_c[:, :]))
                    do(v.tensor_scalar(cnt_i[:, :], cnt_i[:, :], 7, None, ALU.logical_shift_right))
                    do(v.tensor_copy(tiles_c[:, :], cnt_i[:, :]))
                    v.tensor_copy(tiles_b[:, :], tiles_c[:, 0:1].to_broadcast([NK, P])).then_inc(s1_tiles, 1)
                    e.wait_ge(s1_start, 1)
                    do(v.tensor_scalar(start_r[:, :], pb[2][:, 0:NK], float(P), -1.0, ALU.mult, ALU.add))
                    do(v.tensor_tensor(base[:, :], start_r[:, :], pb[1][:, 0:NK], ALU.add))
                    do(v.tensor_copy(end_c[:, :], pb[3][0:NK, 0:1]))
                    v.tensor_scalar(tiles_row[:, :], tiles_row[:, :], end_c[:, 0:1], None, ALU.is_ge).then_inc(s1_past, 1)
                    with e.Fori(0, NK) as k:
                        c.enter(k, 2)
                        do(v.tensor_scalar(hot[:, :], key[:, :], iota_row[:, bass.ds(k, 1)], base[:, bass.ds(k, 1)],
                                           ALU.is_equal, ALU.mult))
                        do(v.tensor_tensor(rank[:, :], rank[:, :], hot[:, :], ALU.add))
                    c.leave(NK)
                    e.wait_ge(s1_blockno, 1)
                    half = NT // 2
                    do(v.tensor_scalar(tb_f[:, 0:half], pb[4][0:1, 0:half], float(NB - 1), None, ALU.min))
                    do(v.tensor_scalar(tb_f[:, half:NT], pb[5][0:1, 0:half], float(NB - 1), None, ALU.min))
                    do(v.tensor_copy(tile_block[:, :], tb_f[:, :]))
                    do(v.tensor_copy(pos_i[:, :], rank[:, :]))
                    do(v.tensor_scalar(lane_i[:, :], pos_i[:, :], P - 1, None, ALU.bitwise_and))
                    do(v.tensor_copy(lane_f[:, :], lane_i[:, :]))
                    do(v.tensor_scalar(pos_i[:, :], pos_i[:, :], 7, None, ALU.logical_shift_right))
                    do(v.tensor_copy(cum[:, :], pos_i[:, :]))
                    do(v.scalar_tensor_tensor(cum[:, :], lane_f[:, :], float(NT), cum[:, :], ALU.mult, ALU.add))
                    e.wait_ge(s1_ld[1], 32)
                    e.wait_ge(s1_ld[2], 32)
                    do(v.tensor_copy(rec[:, :, 1], dst_i[:, :]))
                    do(v.tensor_copy(rec_f[:, :, 2], ew_f[:, :]))
                    do(v.tensor_copy(rec[:, :, 4], cum[:, :]))
                    do(v.tensor_scalar(lane_i[:, :], src_i[:, :], P - 1, None, ALU.bitwise_and))
                    do(v.tensor_copy(lane_f[:, :], lane_i[:, :]))
                    do(v.tensor_scalar(hot[:, :], key[:, :], float(NB), PADLO, ALU.is_equal, ALU.mult))
                    do(v.tensor_tensor(rec_f[:, :, 0], lane_f[:, :], hot[:, :], ALU.add))

        ALM = sb("ALM", [P, NB, 2 * NHEAD])
        MX = sb("MX", [P, NB, NHEAD])
        st = ExitStack()
        with st:
            SLOTS = 4
            stage = [sb(f"stage{q}", [P, 5], I32, ctx=st) for q in range(SLOTS)]
            Wsb = sb("Wsb", [P, KD, D], ctx=st)
            a_b = sb("a_b", [P, 2, D], ctx=st)
            xn = sb("xn", [P, D], ctx=st)
            xnT = sb("xnT", [P, D], ctx=st)
            hrow = sb("hrow", [P, HX], ctx=st)
            hraw = sb("hraw", [P, D], ctx=st)
            hmask = sb("hmask", [P, D], I32, ctx=st)
            hprod = sb("hprod", [P, D], ctx=st)
            s2_w = sem("s2_w")
            s2_se = sem("s2_se")
            s2_dve = sem("s2_dve")
            s2_var = sem("s2_var")
            s2_sqrt = sem("s2_sqrt")
            s2_xn = sem("s2_xn")
            s2_t = sem("s2_t")
            s2_xnT = sem("s2_xnT")
            s2_h = sem("s2_h")
            s2_row = sem("s2_row")
            s2_st = sem("s2_st")
            s2_staged = sem("s2_staged")
            s2_sc = [sem(f"s2_sc{q}") for q in range(SLOTS)]

            with nc.Block() as block:
                @block.gpsimd
                def _(e):
                    def scatter(i, first, slots=SLOTS):
                        for q in range(slots):
                            if not first:
                                e.wait_ge(s2_sc[q], i * 16)
                            g.tensor_copy(stage[q][:, :], blk(rec, i * SLOTS + q)).then_inc(s2_staged, 1)
                            stand(e, s2_staged, i * SLOTS + (q + 1))
                            g.indirect_dma_start(out=sorted_d, out_offset=bass.IndirectOffsetOnAxis(ap=stage[q][:, 4:5], axis=0),
                                                 in_=stage[q][:, 0:4], in_offset=None).then_inc(s2_sc[q], 16)

                    scatter(0, True)
                    with e.Fori(1, EC // SLOTS) as i:
                        scatter(i, False)
                    scatter(EC // SLOTS, False, EC % SLOTS)
                    for q in range(SLOTS):
                        e.wait_ge(s2_sc[q], 16 * (EC // SLOTS + (q < EC % SLOTS)))
                    e.dma_start(SE[:, :, :].rearrange("p t f -> p (t f)"), sorted_d.rearrange("(p t) f -> p (t f)", p=P)).then_inc(s2_se, 16)
                    e.wait_ge(s2_se, 16)

                @block.sync
                def _(e):
                    e.dma_start(Wsb[:, :, :], W.rearrange("(k p) n -> p k n", p=P)).then_inc(s2_w, 16)
                    e.dma_start(a_b[:, 0, :], a_l.rearrange("a h f -> a (h f)").to_broadcast([P, D])).then_inc(s2_w, 16)
                    e.dma_start(a_b[:, 1, :], a_r.rearrange("a h f -> a (h f)").to_broadcast([P, D])).then_inc(s2_w, 16)
                    with e.Fori(0, NB) as b:
                        e.wait_ge(s2_row, b + 1)
                        e.dma_start(gat_d[bass.ds(b * P, P), :], hrow[:, 0:MW]).then_inc(s2_st, 16)
                        e.dma_start(ar_d[bass.ds(b * P, P), :], hrow[:, D:MW]).then_inc(s2_st, 16)
                    e.wait_ge(s2_st, 32 * NB)

                @block.scalar
                def _(e):
                    e.wait_ge(s2_var, 1)
                    s.activation(RS[:, :], rs_t[:, :], ACT.Sqrt).then_inc(s2_sqrt, 1)
                    with e.Fori(0, NB) as b:
                        e.wait_ge(s2_t, b + 1)
                        s.activation(xnT[:, :], pb[0][:, 0:D], ACT.Copy).then_inc(s2_xnT, 1)

                @block.tensor
                def _(e):
                    e.wait_ge(s2_w, 48)
                    with e.Fori(0, NB) as b:
                        e.wait_ge(s2_xn, b + 1)
                        for k in range(KD):
                            last = nc.tensor.transpose(pb[0][:, k * P:(k + 1) * P], xn[:, k * P:(k + 1) * P], ident[:, :])
                        last.then_inc(s2_t, 1)
                        e.wait_ge(s2_xnT, b + 1)
                        for k in range(KD):
                            last = m(pb[1][:, 0:D], xnT[:, k * P:(k + 1) * P], Wsb[:, k, :], start=k == 0, stop=k == KD - 1)
                        last.then_inc(s2_h, 1)

                @block.vector
                def _(e):
                    c = Count(s2_dve)

                    def do(ins):
                        c.up(ins)
                        e.wait_ge(c.sem, c.now)

                    with e.Fori(0, NB) as b:
                        c.enter(b, 3)
                        row_stats(e, c, b)
                    c.leave(NB)
                    do(v.tensor_scalar(rs_t[:, :], MV[:, :, 1], EPS, None, ALU.add))
                    v.reciprocal(rs_t[:, :], rs_t[:, :]).then_inc(s2_var, 1)
                    v.memset(MX[:, :, :], -BIG)
                    e.wait_ge(s2_sqrt, 1)
                    e.wait_ge(s2_w, 48)

                    def table(b, first):
                        normal(xn[:, :], blk(X, b), b).then_inc(s2_xn, 1)
                        e.wait_ge(s2_h, b + 1)
                        do(v.tensor_copy(hraw[:, :], pb[1][:, 0:D]))
                        do(v.tensor_tensor(hmask[:, :], hraw[:, :], hraw[:, :], ALU.is_equal))
                        if not first:
                            e.wait_ge(s2_st, b * 32)
                        c.up(v.memset(hrow[:, 0:D], 0.0))
                        stand(e, c.sem, c.now)
                        do(v.copy_predicated(hrow[:, 0:D], hmask[:, :], hraw[:, :]))
                        do(v.tensor_tensor(hprod[:, :], hrow[:, 0:D], a_b[:, 0, :], ALU.mult))
                        do(v.tensor_reduce(blk(ALM, b)[:, 0:NHEAD], hprod[:, :].rearrange("p (h f) -> p h f", h=NHEAD), AX.X, ALU.add))
                        do(v.tensor_tensor(hprod[:, :], hrow[:, 0:D], a_b[:, 1, :], ALU.mult))
                        v.tensor_reduce(hrow[:, D:MW], hprod[:, :].rearrange("p (h f) -> p h f", h=NHEAD), AX.X, ALU.add).then_inc(s2_row, 1)

                    table(0, True)
                    with e.Fori(1, NB) as b:
                        c.enter(b, 7, 1)
                        table(b, False)
                    c.leave(NB)

        NG = NT // G

        def groups(e, body):
            for i in range(2):
                body(i, i, i == 0, False)
            with e.Fori(1, NG // 2 - 1) as pair:
                for q in range(2):
                    body(pair * 2 + q, q, False, False)
            for i in range(NG - 2, NG):
                body(i, i % 2, False, i == NG - 1)

        def registers(e, name):
            return [e.alloc_register(f"{name}_{j}") for j in range(G)]

        def blocks_of(e, regs, i):
            e.load(regs, tile_block[0:1, bass.ds(i * G, G)])
            return [e.snap(r, min_val=0, max_val=NB - 1) for r in regs]

        def lo(i, j):
            return SE[:, bass.ds(i * G + j, 1), 0].bitcast(F32)

        def dst_of(i):
            return SE[:, bass.ds(i * G, G), 1]

        def gather(e, i, q, slot_idx, slot, table, free, got, copied):
            if not (isinstance(i, int) and i < 2):
                e.wait_ge(free, i - 1)
            g.tensor_copy(slot_idx[q][:, :], dst_of(i)).then_inc(copied, 1)
            stand(e, copied, i + 1)
            for j in range(G):
                g.indirect_dma_start(out=slot[q][:, j, :], out_offset=None, in_=table,
                                     in_offset=bass.IndirectOffsetOnAxis(ap=slot_idx[q][:, j:j + 1], axis=0)).then_inc(got[q], 16)

        def arrived(e, got, i, q):
            e.wait_ge(got[q], 16 * G * (i // 2 + 1) if isinstance(i, int) else (i - q) * (8 * G) + 16 * G)

        st = ExitStack()
        with st:
            idx = [sb(f"ar_idx{q}", [P, G], I32, ctx=st) for q in range(2)]
            ar_e = [sb(f"ar_e{q}", [P, G, NHEAD], ctx=st) for q in range(2)]
            absent = [sb(f"absent{q}", [P, G, P], BF16, ctx=st) for q in range(2)]
            diag = [sb(f"diag{q}", [P, G, NHEAD, P], ctx=st) for q in range(2)]
            red = [sb(f"red{q}", [P, G, NHEAD], ctx=st) for q in range(2)]
            big_id = sb("big_id", [P, NHEAD, P], BF16, ctx=st)
            s3_const = sem("s3_const")
            s3_copied = sem("s3_copied")
            s3_got = [sem(f"s3_got{q}") for q in range(2)]
            s3_absent = sem("s3_absent")
            s3_diag = sem("s3_diag")
            s3_bc = sem("s3_bc")
            s3_red = sem("s3_red")
            s3_max = sem("s3_max")
            s3_m = sem("s3_m")

            with nc.Block() as block:
                @block.gpsimd
                def _(e):
                    groups(e, lambda i, q, first, last: gather(e, i, q, idx, ar_e, ar_d, s3_diag, s3_got, s3_copied))

                @block.scalar
                def _(e):
                    def body(i, q, first, last):
                        arrived(e, s3_got, i, q)
                        if not (isinstance(i, int) and i < 2):
                            e.wait_ge(s3_bc, i - 1)
                        for j in range(G):
                            for h in range(NHEAD):
                                ins = s.activation(diag[q][:, j, h, :], ident[:, :], ACT.Copy, scale=ar_e[q][:, j, h:h + 1])
                        ins.then_inc(s3_diag, 1)
                    groups(e, body)

                @block.tensor
                def _(e):
                    e.wait_ge(s3_const, 1)

                    def body(i, q, first, last):
                        if not (isinstance(i, int) and i < 2):
                            e.wait_ge(s3_red, i - 1)
                        e.wait_ge(s3_absent, i * G + G)
                        e.wait_ge(s3_diag, i + 1)
                        for j in range(G):
                            m(pb[G * q + j][:, :], ones[:, :], diag[q][:, j, :, :].rearrange("p h e -> p (h e)"), start=True, stop=False)
                            ins = m(pb[G * q + j][:, :], absent[q][:, j, :], big_id[:, :, :].rearrange("p h e -> p (h e)"), start=False, stop=True)
                        ins.then_inc(s3_bc, 1)
                    groups(e, body)

                @block.vector
                def _(e):
                    v.tensor_scalar(big_id[:, :, :], ident[:, :].rearrange("p (o e) -> p o e", o=1).to_broadcast([P, NHEAD, P]), BIG, None, ALU.mult).then_inc(s3_const, 1)

                    regs = registers(e, "max_block")

                    def mark(i, j, q):
                        v.tensor_scalar(absent[q][:, j, :], iota_row[:, :], lo(i, j), -1.0, ALU.is_equal, ALU.add).then_inc(s3_absent, 1)

                    for i in range(2):
                        for j in range(G):
                            mark(i, j, i)

                    def body(i, q, first, last):
                        e.wait_ge(s3_bc, i + 1)
                        for j in range(G):
                            ins = v.tensor_reduce(red[q][:, j, :], pb[G * q + j][:, :].rearrange("p (h e) -> p h e", h=NHEAD), AX.X, ALU.max)
                        ins.then_inc(s3_red, 1)
                        blocks = blocks_of(e, regs, i)
                        e.wait_ge(s3_red, i + 1)
                        for j in range(G):
                            if not (first and j == 0):
                                e.wait_ge(s3_max, i * G + j)
                            v.tensor_tensor(blk(MX, blocks[j]), blk(MX, blocks[j]), red[q][:, j, :], ALU.max).then_inc(s3_max, 1)
                            if not (isinstance(i, int) and i >= NG - 2):
                                mark(i + 2, j, q)
                    groups(e, body)
                    e.wait_ge(s3_max, NT)
                    al, mm = ALM[:, :, 0:NHEAD], ALM[:, :, NHEAD:2 * NHEAD]
                    v.tensor_tensor(mm, al, MX[:, :, :], ALU.add).then_inc(s3_m, 1)
                    e.wait_ge(s3_m, 1)
                    v.scalar_tensor_tensor(mm, mm, 0.2, mm, ALU.mult, ALU.max).then_inc(s3_m, 1)
                    v.tensor_scalar(MX[:, :, :], MX[:, :, :], -BIG / 2, None, ALU.is_gt).then_inc(s3_m, 1)
                    e.wait_ge(s3_m, 3)
                    v.tensor_tensor(mm, mm, MX[:, :, :], ALU.mult).then_inc(s3_m, 1)
                    e.wait_ge(s3_m, 4)
                    v.memset(B[:, :], 0.0)

        st = ExitStack()
        with st:
            idx = [sb(f"gat_idx{q}", [P, G], I32, ctx=st) for q in range(2)]
            rows = [sb(f"rows{q}", [P, G, MW], ctx=st) for q in range(2)]
            msg = [sb(f"msg{q}", [P, G, MW], ctx=st) for q in range(2)]
            hot = [sb(f"hot4_{q}", [P, G, P], ctx=st) for q in range(2)]
            hotT = [sb(f"hotT{q}", [P, G, P], ctx=st) for q in range(2)]
            z = [sb(f"z{q}", [P, G, NHEAD], ctx=st) for q in range(2)]
            den = sb("den", [P, NB, NHEAD], ctx=st)
            s4_copied = sem("s4_copied")
            s4_got = [sem(f"s4_got{q}") for q in range(2)]
            s4_hot = sem("s4_hot")
            s4_T = sem("s4_T")
            s4_hotT = sem("s4_hotT")
            s4_look = sem("s4_look")
            s4_z = [sem(f"s4_z{k}") for k in range(4)]
            s4_exp = sem("s4_exp")
            s4_msg = sem("s4_msg")
            s4_sum = sem("s4_sum")
            s4_acc = sem("s4_acc")
            s4_end = sem("s4_end")
            bT, bL, bS = [pb[0], pb[1]], [pb[2], pb[3]], pb[4:8]

            with nc.Block() as block:
                @block.gpsimd
                def _(e):
                    groups(e, lambda i, q, first, last: gather(e, i, q, idx, rows, gat_d, s4_msg, s4_got, s4_copied))

                @block.scalar
                def _(e):
                    def flip(i, q):
                        e.wait_ge(s4_T, i + 1)
                        if not (isinstance(i, int) and i < 2):
                            e.wait_ge(s4_look, i - 1)
                        s.activation(hotT[q][:, :, :].rearrange("p g e -> p (g e)"), bT[q][:, :], ACT.Copy).then_inc(s4_hotT, 1)

                    def body(i, q, first, last):
                        if first:
                            flip(i, q)
                        e.wait_ge(s4_z[3], i + 1)
                        s.activation(msg[q][:, :, D:MW], z[q][:, :, :], ACT.Exp).then_inc(s4_exp, 1)
                        if not last:
                            flip(i + 1, 1 - q)
                    groups(e, body)

                @block.tensor
                def _(e):
                    regs = registers(e, "look_block")

                    def look(i, q):
                        blocks = blocks_of(e, regs, i)
                        e.wait_ge(s4_hot, i * G + G)
                        for j in range(G):
                            ins = nc.tensor.transpose(bT[q][:, j * P:(j + 1) * P], hot[q][:, j, :], ident[:, :])
                        ins.then_inc(s4_T, 1)
                        e.wait_ge(s4_hotT, i + 1)
                        for j in range(G):
                            ins = m(bL[q][:, j * 8:(j + 1) * 8], hotT[q][:, j, :], blk(ALM, blocks[j]), start=True, stop=True)
                        ins.then_inc(s4_look, 1)

                    def body(i, q, first, last):
                        if first:
                            look(i, q)
                        if not last:
                            look(i + 1, 1 - q)
                        e.wait_ge(s4_msg, i + 1)
                        if not first:
                            e.wait_ge(s4_acc, i * G)
                        for j in range(G):
                            ins = m(bS[j][:, 0:MW], hot[q][:, j, :], msg[q][:, j, :], start=True, stop=True)
                        ins.then_inc(s4_sum, 1)
                    groups(e, body)

                @block.vector
                def _(e):
                    regs = registers(e, "sum_block")

                    def mark(i, j, q):
                        v.tensor_scalar(hot[q][:, j, :], iota_row[:, :], lo(i, j), None, ALU.is_equal).then_inc(s4_hot, 1)

                    def take(i, j, first, blocks):
                        if not (first and j == 0):
                            e.wait_ge(s4_acc, i * G + j)
                        b = blocks[j]
                        v.tensor_tensor(blk(acc, b), blk(acc, b), bS[j][:, 0:MW], ALU.add).then_inc(s4_acc, 1)

                    for i in range(2):
                        for j in range(G):
                            mark(i, j, i)

                    def body(i, q, first, last):
                        if not first:
                            blocks = blocks_of(e, regs, i - 1)
                        look = bL[q][:, 0:G * 8].rearrange("p (g f) -> p g f", g=G)
                        arrived(e, s4_got, i, q)
                        e.wait_ge(s4_look, i + 1)
                        v.tensor_tensor(z[q][:, :, :], look[:, :, 0:NHEAD], rows[q][:, :, D:MW], ALU.add).then_inc(s4_z[0], 1)
                        e.wait_ge(s4_z[0], i + 1)
                        v.scalar_tensor_tensor(z[q][:, :, :], z[q][:, :, :], 0.2, z[q][:, :, :], ALU.mult, ALU.max).then_inc(s4_z[1], 1)
                        e.wait_ge(s4_z[1], i + 1)
                        v.tensor_tensor(z[q][:, :, :], z[q][:, :, :], look[:, :, NHEAD:2 * NHEAD], ALU.subtract).then_inc(s4_z[2], 1)
                        e.wait_ge(s4_z[2], i + 1)
                        v.tensor_scalar(z[q][:, :, :], z[q][:, :, :], 0.0, None, ALU.min).then_inc(s4_z[3], 1)
                        e.wait_ge(s4_exp, i + 1)
                        hr, hm = (t[q][:, :, 0:D].rearrange("p g (h f) -> p g h f", h=NHEAD) for t in (rows, msg))
                        for j in range(G):
                            ins = v.tensor_tensor(hm[:, j, :, :], hr[:, j, :, :],
                                                  msg[q][:, j, D:MW].rearrange("p (h o) -> p h o", o=1).to_broadcast([P, NHEAD, FH]), ALU.mult)
                        ins.then_inc(s4_msg, 1)
                        if not first:
                            e.wait_ge(s4_sum, i)
                            if not last:
                                for j in range(G):
                                    mark(i + 1, j, 1 - q)
                            for j in range(G):
                                take(i - 1, j, isinstance(i, int) and i == 1, blocks)
                        if last:
                            blocks = blocks_of(e, regs, i)
                            e.wait_ge(s4_sum, i + 1)
                            for j in range(G):
                                take(i, j, False, blocks)
                    groups(e, body)
                    e.wait_ge(s4_acc, NT)
                    c = Count(s4_end)

                    def do(ins):
                        c.up(ins)
                        e.wait_ge(c.sem, c.now)

                    do(v.tensor_scalar(den[:, :, :], acc[:, :, D:MW], 0.5, None, ALU.max))
                    do(v.reciprocal(den[:, :, :], den[:, :, :]))
                    with e.Fori(0, NB) as b:
                        c.enter(b, 5)
                        hb = blk(acc, b)[:, 0:D].rearrange("p (h f) -> p h f", h=NHEAD)
                        do(v.tensor_tensor(hb, hb, blk(den, b).rearrange("p (h o) -> p h o", o=1).to_broadcast([P, NHEAD, FH]), ALU.mult))
                        c.up(v.tensor_tensor(blk(X, b), blk(X, b), blk(acc, b)[:, 0:D], ALU.add))
                        stand(e, c.sem, c.now)
                        row_stats(e, c, b)
                    c.leave(NB)
                    v.tensor_scalar(rs_t[:, :], MV[:, :, 1], EPS, None, ALU.add)

        hist = B[:, 0:N * KD].rearrange("p (t k) -> p t k", k=KD)
        st = ExitStack()
        with st:
            wih = sb("wih", [P, KD, GATES, P], ctx=st)
            whf = sb("whf", [P, KD, GATES, P], ctx=st)
            w_hi = sb("w_hi", [P, KD, GATES, P], F16, ctx=st)
            w_lo = sb("w_lo", [P, KD, GATES, P], F16, ctx=st)
            ident_b = sb("ident_b", [P, P], BF16, ctx=st)
            bias = sb("bias", [P, GATES], ctx=st)
            bias2 = sb("bias2", [P, GATES], ctx=st)
            xb = sb("xb5", [P, D], ctx=st)
            xstat = sb("xstat", [P, 3], ctx=st)
            xn = sb("xn5", [P, D], ctx=st)
            xnT = sb("xnT5", [P, D], ctx=st)
            xf = [sb(f"xf{q}", [P, P], ctx=st) for q in range(2)]
            xp = [sb(f"xp{r}", [P, 3, P, GATES], BF16, ctx=st) for r in range(2)]
            h_parts = sb("h_parts", [P, KD, 2], F16, ctx=st)
            gate_in = sb("gate_in", [P, 4, KD], ctx=st)
            sig_f = sb("sig_f", [P, KD], ctx=st)
            sig_o = sb("sig_o", [P, KD], ctx=st)
            scan_by = sb("scan_by", [P, KD, 2], ctx=st)
            scan_add = sb("scan_add", [P, KD, 2], ctx=st)
            scan_out = sb("scan_out", [P, KD, 2], ctx=st)
            c_old = scan_out[:, :, 1]
            tan_c = sb("tan_c", [P, KD], ctx=st)
            l5_w = sem("l5_w")
            l5_sqrt = sem("l5_sqrt")
            l5_dve = sem("l5_dve")
            l5_prep = sem("l5_prep")
            l5_scaled = sem("l5_scaled")
            l5_pool = sem("l5_pool")
            l5_xn = sem("l5_xn")
            l5_xT = sem("l5_xT")
            l5_xnT = sem("l5_xnT")
            l5_proj = sem("l5_proj")
            l5_xf = sem("l5_xf")
            l5_xp = sem("l5_xp")
            gates = [sem(f"gates_{n}") for n in "fgio"]
            summed = [sem(f"summed_{n}") for n in "fgio"]
            f_ready = sem("f_ready")
            scan_ready = sem("scan_ready")
            cell = sem("cell")
            tanh_cell = sem("tanh_cell")
            h_first = sem("h_first")
            h_kept = sem("h_kept")
            h_second = sem("h_second")
            bG, bX, bPr = pb[0:4], pb[6], [pb[4], pb[5]]
            U = 8
            PHASES = [2, 2, 2, 2, 2, 2, 1, 1, 1, 1]
            assert sum(PHASES) * U == P and len(PHASES) == GATES + 2

            def run(e, t0, u0, times, r, step):
                with e.Fori(0, times) as i:
                    for j in range(U):
                        step(t0 + (i * U + j), i * U + (u0 + j), r)

            def run_block(e, b, r, step, after):
                start = 0
                for phase, times in enumerate(PHASES):
                    run(e, b * P + start, start, times, r, step)
                    start += times * U
                    after(phase)

            def all_blocks(e, step, begin, chunk, ready):
                def after(b, r):
                    def share(phase):
                        if phase == 0:
                            begin(b)
                        elif phase <= GATES:
                            chunk(b, phase - 1)
                    return share

                begin(0)
                for n in range(GATES):
                    chunk(0, n)
                with e.Fori(0, NB // 2) as i:
                    for r in range(2):
                        b = i * 2 + r
                        ready(b)
                        run_block(e, b, r, step, after(i * 2 + (r + 1), 1 - r))
                ready(NB - 1)
                run(e, (NB - 1) * P, 0, LAST // U, 0, step)
                for u in range(LAST // U * U, LAST):
                    step((NB - 1) * P + u, u, 0)

            assert NB % 2 == 1

            def chunks(b, n):
                return b * GATES + n

            def is_first(b, n, depth):
                return isinstance(b, int) and b * GATES + n < depth

            with nc.Block() as block:
                @block.sync
                def _(e):
                    e.dma_start(whf[:, :, :, :].rearrange("p k g m -> p (k g m)"), W_hh).then_inc(l5_w, 16)
                    e.dma_start(wih[:, :, :, :].rearrange("p k g m -> p (k g m)"), W_ih).then_inc(l5_w, 16)
                    e.dma_start(bias[:, :], b_ih).then_inc(l5_w, 16)
                    e.dma_start(bias2[:, :], b_hh).then_inc(l5_w, 16)
                    e.wait_ge(l5_w, 64)

                @block.scalar
                def _(e):
                    e.wait_ge(l5_dve, 1)
                    s.activation(RS[:, :], rs_t[:, :], ACT.Sqrt).then_inc(l5_sqrt, 1)
                    s.preload_act_table_set("sigmoid_and_others")
                    e.wait_ge(l5_scaled, 1)

                    def step(t, u, r):
                        e.wait_ge(summed[0], t + 1)
                        s.activation(sig_f[:, :], gate_in[:, 0, :], ACT.Sigmoid, scale=1 / W_SCALE).then_inc(f_ready, 1)
                        e.wait_ge(summed[1], t + 1)
                        s.activation(scan_add[:, :, 0], gate_in[:, 1, :], ACT.Tanh, scale=1 / W_SCALE)
                        e.wait_ge(summed[2], t + 1)
                        s.activation(scan_by[:, :, 1], gate_in[:, 2, :], ACT.Sigmoid, scale=1 / W_SCALE).then_inc(scan_ready, 1)
                        e.wait_ge(summed[3], t + 2)
                        s.activation(sig_o[:, :], gate_in[:, 3, :], ACT.Sigmoid, scale=1 / W_SCALE)
                        e.wait_ge(cell, t + 1)
                        s.activation(tan_c[:, :], scan_out[:, :, 1], ACT.Tanh).then_inc(tanh_cell, 1)

                    def begin(b):
                        e.wait_ge(l5_xT, b + 1)
                        s.activation(xnT[:, :], bX[:, 0:D], ACT.Copy).then_inc(l5_xnT, 1)

                    def chunk(b, n):
                        e.wait_ge(l5_proj, chunks(b, n + 1))
                        if not is_first(b, n, 2):
                            e.wait_ge(l5_xp, chunks(b, n - 1))
                        s.activation(xf[n % 2][:, :], bPr[n % 2][:, 0:P], ACT.Identity,
                                     scale=W_SCALE, bias=bias[:, n:n + 1]).then_inc(l5_xf, 1)

                    all_blocks(e, step, begin, chunk, lambda b: None)

                @block.gpsimd
                def _(e):
                    c = Count(l5_pool)

                    def begin(b):
                        if not is_first(b, 0, 1):
                            stand(e, l5_xT, b)
                        g.tensor_copy(xb[:, :], blk(X, b))
                        g.tensor_copy(xstat[:, 0:2], blk(MV, b))
                        c.up(g.tensor_copy(xstat[:, 2:3], RS[:, bass.ds(b, 1)]))
                        stand(e, c.sem, c.now)
                        g.tensor_scalar(xn[:, :], xb[:, :], xstat[:, 0:1], xstat[:, 2:3], ALU.subtract, ALU.mult).then_inc(l5_xn, 1)

                    def chunk(b, n):
                        x_, r = xf[n % 2][:, :], b_buffer[0]
                        stand(e, l5_xf, chunks(b, n + 1))
                        for j in range(2):
                            c.up(g.tensor_copy(xp[r][:, j, :, n], x_))
                            e.wait_ge(c.sem, c.now)
                            c.up(g.tensor_tensor(x_, x_, xp[r][:, j, :, n], ALU.subtract))
                            stand(e, c.sem, c.now)
                        g.tensor_copy(xp[r][:, 2, :, n], x_).then_inc(l5_xp, 1)

                    def prepare(b, r):
                        b_buffer[0] = r
                        begin(b)
                        for n in range(GATES):
                            chunk(b, n)

                    b_buffer = [0]
                    e.wait_ge(l5_sqrt, 1)
                    prepare(0, 0)
                    per = 1 + 4 * GATES
                    with e.Fori(0, NB // 2) as i:
                        c.enter(i, 2 * per)
                        for r in range(2):
                            prepare(i * 2 + (r + 1), 1 - r)
                    c.leave(NB // 2)

                @block.tensor
                def _(e):
                    e.wait_ge(l5_w, 64)

                    def low(n):
                        for h in range(KD):
                            for k in range(KD):
                                m(bG[n][:, h * SUMS:h * SUMS + 1], w_lo[:, k, n * KD + h, :], h_parts[:, k, 0:1],
                                  start=False, stop=False, skip_group_check=True)

                    def high(n):
                        for h in range(KD):
                            for k in range(KD):
                                ins = m(bG[n][:, h * SUMS:h * SUMS + 2], w_hi[:, k, n * KD + h, :], h_parts[:, k, :],
                                        start=False, stop=k == KD - 1, skip_group_check=True)
                        ins.then_inc(gates[n], 1)

                    def step(t, u, r):
                        e.wait_ge(summed[3], t + 1)
                        for n in range(4):
                            m(bG[n][:, 0:KD * SUMS].rearrange("p (h c) -> p c h", c=SUMS)[:, 2:SUMS, :], ident_b[:, :],
                              xp[r][:, :, bass.ds(u, 1), n * KD:(n + 1) * KD].rearrange("p j t h -> p j (t h)"),
                              start=True, stop=False, skip_group_check=True)
                        e.wait_ge(h_first, t + 1)
                        for n in range(3):
                            low(n)
                        e.wait_ge(h_second, t + 1)
                        for n in range(3):
                            high(n)
                        low(3)
                        high(3)

                    def begin(b):
                        e.wait_ge(l5_xn, b + 1)
                        for k in range(KD):
                            ins = nc.tensor.transpose(bX[:, k * P:(k + 1) * P], xn[:, k * P:(k + 1) * P], ident[:, :])
                        ins.then_inc(l5_xT, 1)

                    def chunk(b, n):
                        if n == 0:
                            e.wait_ge(l5_xnT, b + 1)
                        if not is_first(b, n, 2):
                            e.wait_ge(l5_xf, chunks(b, n - 1))
                        for k in range(KD):
                            ins = m(bPr[n % 2][:, 0:P], wih[:, k, n, :], xnT[:, k * P:(k + 1) * P], start=k == 0, stop=k == KD - 1)
                        ins.then_inc(l5_proj, 1)

                    all_blocks(e, step, begin, chunk, lambda b: stand(e, l5_xp, chunks(b, GATES)))

                @block.vector
                def _(e):
                    c = Count(l5_prep)

                    def do(ins):
                        c.up(ins)
                        e.wait_ge(c.sem, c.now)

                    v.reciprocal(rs_t[:, :], rs_t[:, :]).then_inc(l5_dve, 1)
                    do(v.tensor_copy(ident_b[:, :], ident[:, :]))
                    e.wait_ge(l5_w, 64)
                    do(v.tensor_tensor(bias[:, :], bias[:, :], bias2[:, :], ALU.add))
                    v.tensor_scalar(bias[:, :], bias[:, :], W_SCALE, None, ALU.mult).then_inc(l5_scaled, 1)
                    do(v.tensor_scalar(whf[:, :, :, :], whf[:, :, :, :], W_SCALE, None, ALU.mult))
                    do(v.tensor_copy(w_hi[:, :, :, :], whf[:, :, :, :]))
                    do(v.tensor_tensor(w_lo[:, :, :, :], whf[:, :, :, :], w_hi[:, :, :, :], ALU.subtract))
                    c.up(v.memset(scan_by[:, :, :], 0.0))
                    c.up(v.memset(scan_add[:, :, :], 0.0))
                    do(v.memset(scan_out[:, :, :], 0.0))
                    v.memset(gate_in[:, :, :], 0.0).then_inc(summed[3], 1)
                    v.memset(h_parts[:, :, 0], 0.0).then_inc(h_first, 1)
                    v.memset(h_parts[:, :, 1], 0.0).then_inc(h_second, 1)

                    def flat(t):
                        return t[:, :, :].rearrange("p h c -> p (h c)")

                    def step(t, u, r):
                        def add_columns(n):
                            e.wait_ge(gates[n], t + 1)
                            v.tensor_reduce(gate_in[:, n, :], bG[n][:, 0:KD * SUMS].rearrange("p (h c) -> p h c", c=SUMS), AX.X, ALU.add).then_inc(summed[n], 1)

                        for n in range(3):
                            add_columns(n)
                        e.wait_ge(f_ready, t + 1)
                        v.tensor_tensor(scan_add[:, :, 1], sig_f[:, :], c_old, ALU.mult).then_inc(scan_ready, 1)
                        add_columns(3)
                        e.wait_ge(scan_ready, t * 2 + 2)
                        v.tensor_tensor_scan(flat(scan_out), flat(scan_by), flat(scan_add), 0.0, ALU.mult, ALU.add).then_inc(cell, 1)
                        e.wait_ge(tanh_cell, t + 1)
                        hcol = hist[:, bass.ds(t, 1), :].rearrange("p t k -> p (t k)")
                        v.tensor_tensor(h_parts[:, :, 0], sig_o[:, :], tan_c[:, :], ALU.mult).then_inc(h_first, 1)
                        v.tensor_tensor(hcol, sig_o[:, :], tan_c[:, :], ALU.mult).then_inc(h_kept, 1)
                        e.wait_ge(h_kept, t + 1)
                        v.tensor_tensor(h_parts[:, :, 1], hcol, h_parts[:, :, 0], ALU.subtract).then_inc(h_second, 1)

                    all_blocks(e, step, lambda b: None, lambda b, n: None, lambda b: None)

        st = ExitStack()
        with st:
            inc = sb("inc", [P, N, KD], ctx=st)
            gate = sb("gate", [P, N], BF16, ctx=st)
            wl = sb("wl", [P, KD, 2], ctx=st)
            wl_b = sb("wl_b", [P, KD, 2, P], ctx=st)
            bl = sb("bl", [P, 2], ctx=st)
            att = sb("att", [P, 2, KD], ctx=st)
            l1 = sb("l1", [P, 512], ctx=st)
            w6 = sb("w6", [P, 512, KD], ctx=st)
            t6 = sb("t6", [P, 512, KD], ctx=st)
            cp = sb("cp", [P, KD, P], ctx=st)
            s6_cp = sem("s6_cp")
            s6_w = sem("s6_w")
            s6_wb = sem("s6_wb")
            s6_logit = sem("s6_logit")
            s6_dve = sem("s6_dve")
            s6_gate = sem("s6_gate")
            s6_out = sem("s6_out")
            s6_T = sem("s6_T")
            s6_x = sem("s6_x")
            CH = 512
            NCH = N // CH
            REST = N - NCH * CH

            with nc.Block() as block:
                @block.sync
                def _(e):
                    e.dma_start(wl[:, :, :].rearrange("p k l -> p (k l)"), W_lin).then_inc(s6_w, 16)
                    e.dma_start(bl[:, :], b_lin.rearrange("(a l) -> a l", a=1).to_broadcast([P, 2])).then_inc(s6_w, 16)
                    e.dma_start(att[:, 0, :], fw).then_inc(s6_w, 16)
                    e.dma_start(att[:, 1, :], bw).then_inc(s6_w, 16)
                    e.wait_ge(s6_w, 64)

                @block.scalar
                def _(e):
                    e.wait_ge(s6_out, 1)

                    def fetch(b, n, first):
                        if not first:
                            e.wait_ge(s6_T, b)
                        s.activation(cp[:, :, 0:n].rearrange("p k t -> p t k"), hist[:, bass.ds(b * P, n), :], ACT.Copy).then_inc(s6_cp, 1)

                    fetch(0, P, True)
                    with e.Fori(1, NB - 1) as b:
                        fetch(b, P, False)
                    fetch(NB - 1, LAST, False)

                @block.tensor
                def _(e):
                    e.wait_ge(s6_wb, 1)

                    def logits(i, n, first):
                        if not first:
                            e.wait_ge(s6_gate, i)
                        for l in range(2):
                            for k in range(KD):
                                ins = m(pb[l][:, 0:n], wl_b[:, k, l, :], hist[:, bass.ds(i * CH, n), k], start=k == 0, stop=k == KD - 1)
                        ins.then_inc(s6_logit, 1)

                    logits(0, CH, True)
                    with e.Fori(1, NCH) as i:
                        logits(i, CH, False)
                    logits(NCH, REST, False)

                    def back(b, n, first):
                        e.wait_ge(s6_cp, b + 1)
                        if not first:
                            e.wait_ge(s6_x, b)
                        for k in range(KD):
                            ins = nc.tensor.transpose(pb[2][0:n, k * P:(k + 1) * P], cp[:, k, 0:n], ident[:, :])
                        ins.then_inc(s6_T, 1)

                    back(0, P, True)
                    with e.Fori(1, NB - 1) as b:
                        back(b, P, False)
                    back(NB - 1, LAST, False)

                @block.vector
                def _(e):
                    c = Count(s6_dve)

                    def do(ins):
                        c.up(ins)
                        e.wait_ge(c.sem, c.now)

                    e.wait_ge(s6_w, 64)
                    v.tensor_copy(wl_b[:, :, :, :].rearrange("p k l m -> p (k l) m"),
                                  wl[:, :, :].rearrange("p k (l o) -> p (k l) o", o=1).to_broadcast([P, KD * 2, P])).then_inc(s6_wb, 1)

                    def sums(i, n, first):
                        t0 = i * CH
                        e.wait_ge(s6_logit, i + 1)
                        do(v.tensor_scalar(l1[:, 0:n], pb[1][:, 0:n], bl[:, 1:2], None, ALU.add))
                        v.scalar_tensor_tensor(gate[:, bass.ds(t0, n)], pb[0][:, 0:n], bl[:, 0:1], l1[:, 0:n], ALU.add, ALU.is_lt).then_inc(s6_gate, 1)
                        e.wait_ge(s6_gate, i + 1)
                        for k in range(KD):
                            c.up(v.tensor_tensor(w6[:, 0:n, k], gate[:, bass.ds(t0, n)], hist[:, bass.ds(t0, n), k], ALU.mult))
                        e.wait_ge(c.sem, c.now)
                        for k in range(KD):
                            prev = 0.0 if first else inc[:, bass.ds(t0 - 1, 1), k]
                            c.up(v.tensor_tensor_scan(inc[:, bass.ds(t0, n), k], w6[:, 0:n, k], t6[:, 0:n, k], prev, ALU.add, ALU.add))
                        e.wait_ge(c.sem, c.now)

                    do(v.memset(t6[:, :, :], 0.0))
                    sums(0, CH, True)
                    with e.Fori(1, NCH) as i:
                        c.enter(i, 5, 1)
                        sums(i, CH, False)
                    c.leave(NCH)
                    sums(NCH, REST, False)

                    def outp(t0, n):
                        for k in range(KD):
                            c.up(v.tensor_tensor(w6[:, 0:n, k], gate[:, bass.ds(t0, n)], hist[:, bass.ds(t0, n), k], ALU.mult))
                        e.wait_ge(c.sem, c.now)
                        do(v.tensor_tensor(w6[:, 0:n, :], inc[:, bass.ds(t0, n), :], w6[:, 0:n, :], ALU.subtract))
                        for k in range(KD):
                            c.up(v.tensor_scalar(w6[:, 0:n, k], w6[:, 0:n, k], att[:, 0, k:k + 1], None, ALU.mult))
                            c.up(v.tensor_scalar(t6[:, 0:n, k], inc[:, bass.ds(t0, n), k], inc[:, N - 1:N, k], att[:, 1, k:k + 1], ALU.subtract, ALU.mult))
                        e.wait_ge(c.sem, c.now)
                        do(v.tensor_tensor(w6[:, 0:n, :], w6[:, 0:n, :], t6[:, 0:n, :], ALU.subtract))
                        do(v.scalar_tensor_tensor(hist[:, bass.ds(t0, n), :], hist[:, bass.ds(t0, n), :], 2.0, w6[:, 0:n, :], ALU.mult, ALU.add))

                    with e.Fori(0, NCH) as i:
                        c.enter(i, 9)
                        outp(i * CH, CH)
                    c.leave(NCH)
                    outp(NCH * CH, REST)
                    v.memset(l1[:, 0:1], 0.0).then_inc(s6_out, 1)

                    def rows(b, n):
                        e.wait_ge(s6_T, b + 1)
                        xb = blk(X, b) if n == P else X[0:n, NB - 1, :]
                        v.tensor_tensor(xb, xb, pb[2][0:n, 0:D], ALU.add).then_inc(s6_x, 1)
                        stand(e, s6_x, b + 1)
                        row_stats(e, c, b)

                    with e.Fori(0, NB - 1) as b:
                        c.enter(b, 3)
                        rows(b, P)
                    c.leave(NB - 1)
                    rows(NB - 1, LAST)
                    do(v.tensor_scalar(rs_t[:, :], MV[:, :, 1], EPS, None, ALU.add))
                    do(v.reciprocal(rs_t[:, :], rs_t[:, :]))

        featB = acc[:, :, 0:D]
        st = ExitStack()
        with st:
            mean_b = sb("mean_b", [P, D], ctx=st)
            scale_b = sb("scale_b", [P, D], ctx=st)
            sq = [sb(f"sq{q}", [P, D], ctx=st) for q in range(2)]
            s7_sqrt = sem("s7_sqrt")
            s7_f = sem("s7_f")
            s7_sum = sem("s7_sum")
            s7_mean = sem("s7_mean")
            s7_cen = sem("s7_cen")
            s7_sq = sem("s7_sq")
            s7_ssq = sem("s7_ssq")
            s7_var = sem("s7_var")
            s7_std = sem("s7_std")
            s7_dve = sem("s7_dve")
            s7_feat = sem("s7_feat")
            s7_st = sem("s7_st")

            with nc.Block() as block:
                @block.sync
                def _(e):
                    e.wait_ge(s7_feat, 1)
                    e.dma_start(feat_d.rearrange("(b p) d -> p b d", p=P), featB).then_inc(s7_st, 16)
                    e.wait_ge(s7_st, 16)

                @block.scalar
                def _(e):
                    s.activation(RS[:, :], rs_t[:, :], ACT.Sqrt).then_inc(s7_sqrt, 1)
                    e.wait_ge(s7_cen, 1)

                    def square(b, q):
                        if not (isinstance(b, int) and b < 2):
                            e.wait_ge(s7_ssq, b - 1)
                        s.activation(sq[q][:, :], blk(acc, b)[:, 0:D], ACT.Square).then_inc(s7_sq, 1)

                    square(0, 0)
                    square(1, 1)
                    with e.Fori(1, NB // 2) as i:
                        for q in range(2):
                            square(i * 2 + q, q)
                    square(NB - 1, 0)
                    e.wait_ge(s7_var, 1)
                    s.activation(scale_b[:, :], scale_b[:, :], ACT.Sqrt).then_inc(s7_std, 1)

                @block.tensor
                def _(e):
                    def total(b, start, stop):
                        e.wait_ge(s7_f, b + 1)
                        m(pb[0][:, 0:D], ones[:, :], blk(acc, b)[:, 0:D], start=start, stop=stop).then_inc(s7_sum, 1)

                    total(0, True, False)
                    with e.Fori(1, NB - 1) as b:
                        total(b, False, False)
                    total(NB - 1, False, True)

                    def squares(b, q, rows, start, stop):
                        e.wait_ge(s7_sq, b + 1)
                        m(pb[1][:, 0:D], ones[0:rows, :], sq[q][0:rows, :], start=start, stop=stop).then_inc(s7_ssq, 1)

                    squares(0, 0, P, True, False)
                    squares(1, 1, P, False, False)
                    with e.Fori(1, NB // 2) as i:
                        for q in range(2):
                            squares(i * 2 + q, q, P, False, False)
                    squares(NB - 1, 0, LAST, False, True)

                @block.vector
                def _(e):
                    e.wait_ge(s7_sqrt, 1)
                    with e.Fori(0, NB) as b:
                        normal(blk(acc, b)[:, 0:D], blk(X, b), b).then_inc(s7_f, 1)
                    e.wait_ge(s7_sum, NB)
                    v.tensor_scalar(mean_b[:, :], pb[0][:, 0:D], 1.0 / N, None, ALU.mult).then_inc(s7_mean, 1)
                    e.wait_ge(s7_mean, 1)
                    e.wait_ge(s7_f, NB)

                    def over_rows(t):
                        return t[:, :].rearrange("p (o d) -> p o d", o=1).to_broadcast([P, NB, D])

                    v.tensor_tensor(featB, featB, over_rows(mean_b), ALU.subtract).then_inc(s7_cen, 1)
                    e.wait_ge(s7_ssq, NB)
                    v.tensor_scalar(scale_b[:, :], pb[1][:, 0:D], 1.0 / (N - 1), None, ALU.mult).then_inc(s7_var, 1)
                    e.wait_ge(s7_std, 1)
                    v.tensor_scalar(scale_b[:, :], scale_b[:, :], 1e-4, None, ALU.add).then_inc(s7_dve, 1)
                    e.wait_ge(s7_dve, 1)
                    v.reciprocal(scale_b[:, :], scale_b[:, :]).then_inc(s7_dve, 1)
                    e.wait_ge(s7_dve, 2)
                    e.wait_ge(s7_cen, 1)
                    v.tensor_tensor(featB, featB, over_rows(scale_b), ALU.mult).then_inc(s7_feat, 1)
                    e.wait_ge(s7_st, 16)
                    v.memset(B[:, :], 0.0)

        st = ExitStack()
        with st:
            idx = [sb(f"f_idx{q}", [P, G], I32, ctx=st) for q in range(2)]
            fe = [sb(f"fe{q}", [P, G, D], ctx=st) for q in range(2)]
            hot = [sb(f"hot8_{q}", [P, G, P], ctx=st) for q in range(2)]
            s8_copied = sem("s8_copied")
            s8_got = [sem(f"s8_got{q}") for q in range(2)]
            s8_hot = sem("s8_hot")
            s8_sum = sem("s8_sum")
            s8_acc = sem("s8_acc")

            with nc.Block() as block:
                @block.gpsimd
                def _(e):
                    groups(e, lambda i, q, first, last: gather(e, i, q, idx, fe, feat_d, s8_sum, s8_got, s8_copied))

                @block.tensor
                def _(e):
                    def body(i, q, first, last):
                        e.wait_ge(s8_hot, i * G + G)
                        arrived(e, s8_got, i, q)
                        if not (isinstance(i, int) and i < 2):
                            e.wait_ge(s8_acc, i * G - G)
                        for j in range(G):
                            ins = m(pb[G * q + j][:, 0:D], hot[q][:, j, :], fe[q][:, j, :], start=True, stop=True)
                        ins.then_inc(s8_sum, 1)
                    groups(e, body)

                @block.vector
                def _(e):
                    regs = registers(e, "f_block")

                    def mark(i, j, q):
                        v.tensor_scalar(hot[q][:, j, :], iota_row[:, :], lo(i, j),
                                        SE[:, bass.ds(i * G + j, 1), 2].bitcast(F32), ALU.is_equal, ALU.mult).then_inc(s8_hot, 1)

                    for i in range(2):
                        for j in range(G):
                            mark(i, j, i)

                    def body(i, q, first, last):
                        blocks = blocks_of(e, regs, i)
                        e.wait_ge(s8_sum, i + 1)
                        for j in range(G):
                            if not (first and j == 0):
                                e.wait_ge(s8_acc, i * G + j)
                            b = blocks[j]
                            v.tensor_tensor(blk(acc, b)[:, 0:D], blk(acc, b)[:, 0:D], pb[G * q + j][:, 0:D], ALU.add).then_inc(s8_acc, 1)
                            if not (isinstance(i, int) and i >= NG - 2):
                                mark(i + 2, j, q)
                    groups(e, body)

        st = ExitStack()
        with st:
            W2sb = sb("W2sb", [P, NE * HC, D], ctx=st)
            Wrsb = sb("Wrsb", [P, KD, NE], ctx=st)
            br_b = sb("br_b", [P, NE], ctx=st)
            gam = sb("gam", [P, KD], ctx=st)
            bet = sb("bet", [P, KD], ctx=st)
            b1sb = sb("b1sb", [P, NE * HC], ctx=st)
            b2sb = sb("b2sb", [NE, D], ctx=st)
            MV2 = sb("MV2", [P, NB, 2], ctx=st)
            RS2 = sb("RS2", [P, NB], ctx=st)
            sel = sb("sel", [NE, NE, P], ctx=st)
            s9_w = sem("s9_w")
            st9 = ExitStack()
            with st9:
                Wgsb = sb("Wgsb", [P, KD, D], ctx=st9)
                bg_b = sb("bg_b", [P, D], ctx=st9)
                sup = sb("sup", [P, D], ctx=st9)
                supT = sb("supT", [P, D], ctx=st9)
                t9 = sb("t9", [P, D], ctx=st9)
                s9_g = sem("s9_g")
                s9_cp = sem("s9_cp")
                s9_T = sem("s9_T")
                s9_supT = sem("s9_supT")
                s9_o = sem("s9_o")
                s9_dve = sem("s9_dve")
                s9_free = sem("s9_free")
                s9_var = sem("s9_var")
                s9_sqrt = sem("s9_sqrt")
                s9_sel = sem("s9_sel")

                with nc.Block() as block:
                    @block.sync
                    def _(e):
                        e.dma_start(Wgsb[:, :, :], Wg.rearrange("(k p) n -> p k n", p=P)).then_inc(s9_g, 16)
                        e.dma_start(bg_b[:, :], bg.rearrange("(a n) -> a n", a=1).to_broadcast([P, D])).then_inc(s9_g, 16)
                        e.dma_start(W2sb[:, :, :], W2.rearrange("e (c p) n -> p (e c) n", p=P)).then_inc(s9_w, 16)
                        e.dma_start(Wrsb[:, :, :], Wr.rearrange("(k p) n -> p k n", p=P)).then_inc(s9_w, 16)
                        e.dma_start(br_b[:, :], br.rearrange("(a n) -> a n", a=1).to_broadcast([P, NE])).then_inc(s9_w, 16)
                        e.dma_start(gam[:, :], gamma).then_inc(s9_w, 16)
                        e.dma_start(bet[:, :], beta).then_inc(s9_w, 16)
                        e.dma_start(b1sb[:, :], b1).then_inc(s9_w, 16)
                        e.dma_start(b2sb[:, :], b2).then_inc(s9_w, 16)
                        e.wait_ge(s9_g, 32)
                        e.wait_ge(s9_w, 16 * 7)

                    @block.gpsimd
                    def _(e):
                        g.memset(sel[:, :, :], 0.0).then_inc(s9_sel, 1)
                        e.wait_ge(s9_sel, 1)
                        g.affine_select(out=sel[:, :, :], in_=sel[:, :, :], compare_op=ALU.not_equal, fill=1.0,
                                        base=0, pattern=[[-1, NE], [0, P]], channel_multiplier=1)

                    @block.scalar
                    def _(e):
                        def one(b, first):
                            if not first:
                                e.wait_ge(s9_T, b)
                            s.activation(sup[:, :], blk(acc, b)[:, 0:D], ACT.Copy).then_inc(s9_cp, 1)
                            e.wait_ge(s9_T, b + 1)
                            if not first:
                                e.wait_ge(s9_o, b)
                            s.activation(supT[:, :], pb[0][:, 0:D], ACT.Copy).then_inc(s9_supT, 1)

                        one(0, True)
                        with e.Fori(1, NB) as b:
                            one(b, False)
                        for k, r in ((1, RS), (2, RS2)):
                            e.wait_ge(s9_var, k)
                            s.activation(r[:, :], rs_t[:, :], ACT.Sqrt).then_inc(s9_sqrt, 1)

                    @block.tensor
                    def _(e):
                        e.wait_ge(s9_g, 32)

                        def one(b, first):
                            e.wait_ge(s9_cp, b + 1)
                            if not first:
                                e.wait_ge(s9_supT, b)
                            for k in range(KD):
                                ins = nc.tensor.transpose(pb[0][:, k * P:(k + 1) * P], sup[:, k * P:(k + 1) * P], ident[:, :])
                            ins.then_inc(s9_T, 1)
                            e.wait_ge(s9_supT, b + 1)
                            if not first:
                                e.wait_ge(s9_free, b)
                            for k in range(KD):
                                ins = m(pb[1][:, 0:D], supT[:, k * P:(k + 1) * P], Wgsb[:, k, :], start=k == 0, stop=k == KD - 1)
                            ins.then_inc(s9_o, 1)

                        one(0, True)
                        with e.Fori(1, NB) as b:
                            one(b, False)

                    @block.vector
                    def _(e):
                        c = Count(s9_dve)

                        def do(ins):
                            c.up(ins)
                            e.wait_ge(c.sem, c.now)

                        e.wait_ge(s9_g, 32)
                        with e.Fori(0, NB) as b:
                            c.enter(b, 4)
                            e.wait_ge(s9_o, b + 1)
                            v.tensor_tensor(t9[:, :], pb[1][:, 0:D], bg_b[:, :], ALU.add).then_inc(s9_free, 1)
                            e.wait_ge(s9_free, b + 1)
                            c.up(v.tensor_tensor(blk(X, b), blk(X, b), t9[:, :], ALU.add))
                            stand(e, c.sem, c.now)
                            row_stats(e, c, b)
                        c.leave(NB)
                        do(v.tensor_scalar(rs_t[:, :], MV[:, :, 1], EPS, None, ALU.add))
                        v.reciprocal(rs_t[:, :], rs_t[:, :]).then_inc(s9_var, 1)
                        e.wait_ge(s9_sqrt, 1)
                        with e.Fori(0, NB) as b:
                            c.enter(b, 4)
                            do(normal(t9[:, :], blk(X, b), b))
                            c.up(v.bn_stats(stat6[:, 0, :], t9[:, :]))
                            stand(e, c.sem, c.now)
                            do(v.bn_aggr(mv1[:, :], stat6[:, 0, :]))
                            do(v.tensor_copy(blk(MV2, b), mv1[:, :]))
                        c.leave(NB)
                        do(v.tensor_scalar(rs_t[:, :], MV2[:, :, 1], EPS, None, ALU.add))
                        v.reciprocal(rs_t[:, :], rs_t[:, :]).then_inc(s9_var, 1)

            W1sb = B[:, 0:NE * KD * HID].rearrange("p (e k n) -> p e k n", e=NE, k=KD)
            xn4 = sb("xn4", [P, G, D], ctx=st)
            xnT = sb("xnT10", [P, KD, G * P], ctx=st)
            lg = sb("lg", [P, G, NE], ctx=st)
            mx8 = sb("mx8", [P, G, 8], ctx=st)
            ix8 = sb("ix8", [P, G, 8], U32, ctx=st)
            ixf = sb("ixf", [P, G, 8], ctx=st)
            d21 = sb("d21", [P, G, 1], ctx=st)
            wts = sb("wts", [P, G, 2], ctx=st)
            wf = sb("wf", [P, G, NE], ctx=st)
            wf2 = sb("wf2", [P, G, NE], ctx=st)
            wT = sb("wT", [NE, G * P], ctx=st)
            hT = [sb(f"hT{q}", [P, G * P], ctx=st) for q in range(2)]
            yS = sb("yS", [P, KD, G * P], ctx=st)
            t_w1 = sem("t_w1")
            t_dve = sem("t_dve")
            t_xn = sem("t_xn")
            t_T = sem("t_T")
            t_xnT = sem("t_xnT")
            t_lg = sem("t_lg")
            t_d21 = sem("t_d21")
            t_exp = sem("t_exp")
            t_wf = sem("t_wf")
            t_wTp = sem("t_wTp")
            t_wT = sem("t_wT")
            t_wb = sem("t_wb")
            t_H = sem("t_H")
            t_gelu = sem("t_gelu")
            t_hw = sem("t_hw")
            t_Y = sem("t_Y")
            t_yS = sem("t_yS")
            t_back = sem("t_back")
            t_x = sem("t_x")
            t_out = sem("t_out")
            NU = NE * HC
            bH, bW, bY, bL, bwT = [pb[0], pb[1]], [pb[2], pb[3]], [pb[4], pb[5]], pb[6], pb[7]
            NGB = NB // G
            assert NB == NGB * G + 1

            with nc.Block() as block:
                @block.sync
                def _(e):
                    e.dma_start(W1sb, W1.rearrange("e (k p) n -> p e k n", p=P)).then_inc(t_w1, 16)
                    with e.Fori(0, NGB) as i:
                        e.wait_ge(t_x, i + 1)
                        e.dma_start(out[bass.ds(i * (G * P), G * P), :].rearrange("(b p) d -> p b d", p=P), X[:, bass.ds(i * G, G), :]).then_inc(t_out, 16)
                    e.wait_ge(t_x, NGB + 1)
                    e.dma_start(out[(NB - 1) * P:N, :], X[0:LAST, NB - 1, :]).then_inc(t_out, 16)
                    e.wait_ge(t_out, 16 * (NGB + 1))
                    e.wait_ge(t_w1, 16)

                @block.scalar
                def _(e):
                    def body(i, nb):
                        n = nb * P
                        e.wait_ge(t_d21, i + 1)
                        s.activation(wts[:, 0:nb, 1:2], d21[:, 0:nb, :], ACT.Exp).then_inc(t_exp, 1)
                        e.wait_ge(t_wTp, i + 1)
                        s.activation(wT[:, 0:n], bwT[0:NE, 0:n], ACT.Copy).then_inc(t_wT, 1)
                        for u in range(NU):
                            e.wait_ge(t_H, i * NU + (u + 1))
                            if not (isinstance(i, int) and i == 0 and u < 2):
                                e.wait_ge(t_Y, i * NU + (u - 1))
                            s.activation(hT[u % 2][:, 0:n], bH[u % 2][:, 0:n], ACT.Gelu, bias=b1sb[:, u:u + 1]).then_inc(t_gelu, 1)
                        e.wait_ge(t_Y, i * NU + NU)
                        s.activation(yS[:, 0, 0:n], bY[0][:, 0:n], ACT.Copy)
                        s.activation(yS[:, 1, 0:n], bY[1][:, 0:n], ACT.Copy).then_inc(t_yS, 1)

                    body(0, G)
                    with e.Fori(1, NGB) as i:
                        body(i, G)
                    body(NGB, 1)

                @block.tensor
                def _(e):
                    e.wait_ge(t_w1, 16)

                    def body(i, nb):
                        n = nb * P
                        e.wait_ge(t_xn, i + 1)
                        for k in range(KD):
                            for r in range(nb):
                                ins = nc.tensor.transpose(bH[k][:, r * P:(r + 1) * P], xn4[:, r, k * P:(k + 1) * P], ident[:, :])
                        ins.then_inc(t_T, 1)
                        e.wait_ge(t_xnT, i + 1)
                        for r in range(nb):
                            for k in range(KD):
                                ins = m(bL[:, r * NE:(r + 1) * NE], xnT[:, k, r * P:(r + 1) * P], Wrsb[:, k, :], start=k == 0, stop=k == KD - 1)
                        ins.then_inc(t_lg, 1)
                        e.wait_ge(t_wf, i + 1)
                        for r in range(nb):
                            ins = nc.tensor.transpose(bwT[0:NE, r * P:(r + 1) * P], wf[:, r, :], ident[:, :])
                        ins.then_inc(t_wTp, 1)
                        e.wait_ge(t_wT, i + 1)
                        for d in range(KD):
                            m(bY[d][:, 0:n], b2sb[:, d * P:(d + 1) * P], wT[:, 0:n], start=True, stop=False, skip_group_check=True)

                        def down(u):
                            e.wait_ge(t_hw, i * NU + (u + 1))
                            for d in range(KD):
                                ins = m(bY[d][:, 0:n], W2sb[:, u, d * P:(d + 1) * P], hT[u % 2][:, 0:n], start=False, stop=u == NU - 1, skip_group_check=True)
                            ins.then_inc(t_Y, 1)

                        for u in range(NU):
                            x_, hc = u // HC, u % HC
                            if hc == 0:
                                m(bW[x_ % 2][:, 0:n], sel[:, x_, :], wT[:, 0:n], start=True, stop=True).then_inc(t_wb, 1)
                            if u >= 2:
                                e.wait_ge(t_gelu, i * NU + (u - 1))
                            for k in range(KD):
                                ins = m(bH[u % 2][:, 0:n], W1sb[:, x_, k, hc * P:(hc + 1) * P], xnT[:, k, 0:n], start=k == 0, stop=k == KD - 1)
                            ins.then_inc(t_H, 1)
                            if u >= 1:
                                down(u - 1)
                        down(NU - 1)
                        e.wait_ge(t_yS, i + 1)
                        for r in range(nb):
                            for d in range(KD):
                                ins = nc.tensor.transpose(bH[r // 2][:, (r % 2) * D + d * P:(r % 2) * D + (d + 1) * P], yS[:, d, r * P:(r + 1) * P], ident[:, :])
                        ins.then_inc(t_back, 1)

                    body(0, G)
                    with e.Fori(1, NGB) as i:
                        body(i, G)
                    body(NGB, 1)

                @block.vector
                def _(e):
                    c = Count(t_dve)

                    def do(ins):
                        c.up(ins)
                        e.wait_ge(c.sem, c.now)

                    def body(i, nb):
                        n = nb * P
                        for r in range(nb):
                            b = i * G + r
                            c.up(normal(xn4[:, r, :], blk(X, b), b))
                        e.wait_ge(c.sem, c.now)
                        for r in range(nb):
                            b = i * G + r
                            ins = v.tensor_scalar(xn4[:, r, :], xn4[:, r, :], MV2[:, bass.ds(b, 1), 0], RS2[:, bass.ds(b, 1)], ALU.subtract, ALU.mult)
                        ins.then_inc(t_xn, 1)
                        e.wait_ge(t_T, i + 1)
                        for k in range(KD):
                            ins = v.tensor_scalar(xnT[:, k, 0:n], bH[k][:, 0:n], gam[:, k:k + 1], bet[:, k:k + 1], ALU.mult, ALU.add)
                        ins.then_inc(t_xnT, 1)
                        e.wait_ge(t_lg, i + 1)
                        do(v.tensor_tensor(lg[:, 0:nb, :], bL[:, 0:nb * NE].rearrange("p (r x) -> p r x", r=nb),
                                           br_b[:, :].rearrange("p (o x) -> p o x", o=1).to_broadcast([P, nb, NE]), ALU.add))
                        stand(e, c.sem, c.now)
                        for r in range(nb):
                            c.up(v.max(mx8[:, r, :], lg[:, r, :]))
                        stand(e, c.sem, c.now)
                        for r in range(nb):
                            c.up(v.max_index(ix8[:, r, :], mx8[:, r, :], lg[:, r, :]))
                        v.tensor_tensor(d21[:, 0:nb, :], mx8[:, 0:nb, 1:2], mx8[:, 0:nb, 0:1], ALU.subtract).then_inc(t_d21, 1)
                        e.wait_ge(c.sem, c.now)
                        do(v.tensor_copy(ixf[:, 0:nb, :], ix8[:, 0:nb, :]))
                        e.wait_ge(t_exp, i + 1)
                        do(v.tensor_scalar(wts[:, 0:nb, 0:1], wts[:, 0:nb, 1:2], 1.0, None, ALU.add))
                        do(v.reciprocal(wts[:, 0:nb, 0:1], wts[:, 0:nb, 0:1]))
                        do(v.tensor_tensor(wts[:, 0:nb, 1:2], wts[:, 0:nb, 1:2], wts[:, 0:nb, 0:1], ALU.mult))
                        for r in range(nb):
                            c.up(v.tensor_scalar(wf[:, r, :], iota_row[:, 0:NE], ixf[:, r, 0:1], wts[:, r, 0:1], ALU.is_equal, ALU.mult))
                            c.up(v.tensor_scalar(wf2[:, r, :], iota_row[:, 0:NE], ixf[:, r, 1:2], wts[:, r, 1:2], ALU.is_equal, ALU.mult))
                        e.wait_ge(c.sem, c.now)
                        v.tensor_tensor(wf[:, 0:nb, :], wf[:, 0:nb, :], wf2[:, 0:nb, :], ALU.add).then_inc(t_wf, 1)
                        for u in range(NU):
                            if u % HC == 0:
                                e.wait_ge(t_wb, i * NE + (u // HC + 1))
                            e.wait_ge(t_gelu, i * NU + (u + 1))
                            v.tensor_tensor(hT[u % 2][:, 0:n], hT[u % 2][:, 0:n], bW[(u // HC) % 2][:, 0:n], ALU.mult).then_inc(t_hw, 1)
                        e.wait_ge(t_back, i + 1)
                        for r in range(nb):
                            xb = blk(X, i * G + r)
                            ins = v.tensor_tensor(xb, xb, bH[r // 2][:, (r % 2) * D:(r % 2 + 1) * D], ALU.add)
                        ins.then_inc(t_x, 1)

                    per = G + 1 + G + G + 1 + 3 + 2 * G
                    body(0, G)
                    with e.Fori(1, NGB) as i:
                        c.enter(i, per, 1)
                        body(i, G)
                    c.leave(NGB)
                    body(NGB, 1)


_INS = ["x", "src", "dst", "edge_weight", "L0_gnn_W", "L0_gnn_a_l", "L0_gnn_a_r", "L0_ffn_W_ih", "L0_ffn_W_hh",
        "L0_ffn_b_ih", "L0_ffn_b_hh", "L0_ffn_W_lin", "L0_ffn_b_lin", "L0_ffn_fw_att", "L0_ffn_bw_att",
        "L1_gnn_weight", "L1_gnn_bias", "L1_ffn_gamma", "L1_ffn_beta", "L1_ffn_Wr", "L1_ffn_br",
        "L1_ffn_W1", "L1_ffn_b1", "L1_ffn_W2", "L1_ffn_b2"]


GATE_ORDER = (1, 2, 0, 3)


def _columns(w):
    w = np.concatenate([w[i * D:(i + 1) * D] for i in GATE_ORDER])
    return w.T.reshape(KD, P, GATES, P).transpose(1, 0, 2, 3).reshape(P, KD * GATES * P)


def _halves(a):
    return np.asarray(a).reshape(-1, P).T


def _laid_out(inputs):
    a = {n: np.asarray(inputs[n]) for n in _INS}
    for n in ("L0_ffn_W_ih", "L0_ffn_W_hh"):
        a[n] = _columns(a[n])
    for n in ("L0_ffn_b_ih", "L0_ffn_b_hh"):
        a[n] = _halves(np.concatenate([a[n][i * D:(i + 1) * D] for i in GATE_ORDER]))
    a["L0_ffn_W_lin"] = a["L0_ffn_W_lin"].T.reshape(KD, P, 2).transpose(1, 0, 2).reshape(P, KD * 2)
    for n in ("L0_ffn_fw_att", "L0_ffn_bw_att", "L1_ffn_gamma", "L1_ffn_beta"):
        a[n] = _halves(a[n].reshape(-1))
    a["L1_ffn_b1"] = _halves(a["L1_ffn_b1"].reshape(-1))
    return {n: np.ascontiguousarray(b) for n, b in a.items()}


def kernel(**inputs):
    import concourse.bacc as _bacc
    from concourse import mybir as _mybir
    from concourse.bass_utils import run_bass_kernel_spmd as _run

    nc = _bacc.Bacc("TRN2", target_bir_lowering=False, num_devices=1)
    arrays, args = {}, []
    for name, a in _laid_out(inputs).items():
        arrays[f"in_{name}"] = a
        args.append(nc.dram_tensor(f"in_{name}", a.shape, _mybir.dt.from_np(a.dtype), kind="ExternalInput").ap())
    out = nc.dram_tensor("out_0", (N, D), F32, kind="ExternalOutput").ap()
    build(nc, *args, out)
    r = _run(nc, [arrays], core_ids=[0])
    return r.results[0]["out_0"]
```
